# Optimizing a Trainium2 kernel written in Bass

```python
import numpy as np
import jax
import jax.numpy as jnp

def _softmax(x, axis=-1):
    return jax.nn.softmax(x, axis=axis)

def _gelu(x):
    return jax.nn.gelu(x, approximate=True)

def _silu(x):
    return jax.nn.silu(x)

def _sigmoid(x):
    return jax.nn.sigmoid(x)

def _layernorm(x, axis=-1, eps=1e-05):
    m = jnp.mean(x, axis=axis, keepdims=True)
    v = jnp.var(x, axis=axis, keepdims=True)
    return (x - m) / jnp.sqrt(v + eps)

def _scatter_add(tgt, idx, src, axis=0):
    return tgt.at[idx].add(src)

def _segment_sum(src, seg, n):
    return jax.ops.segment_sum(src, seg, n)
kernel_name = 'mk_vit_tower_cls_d1_tok_img1024_r4_055836'

def setup_inputs(seed: int=0):
    np.random.seed(seed)
    _w = jnp.asarray

    def _rec_inputs():
        import jax
        import jax.numpy as jnp
        _rk = jax.random.key(seed)
        x = -0.00016672 + 0.999947 * jax.random.normal(jax.random.fold_in(_rk, 1), (32, 3, 96, 96), jnp.float32)
        cls_tok = 0.02 * jax.random.normal(jax.random.fold_in(_rk, 5), (1, 1, 256), jnp.float32)
        return (x, cls_tok)
    x, cls_tok = _rec_inputs()

    def _L0_tok_setup():
        import jax, jax.numpy as jnp
        import numpy as np
        DIM = 256
        IMG = 96
        P = 16
        C = 3
        TEMP = 10000.0
        EPS = 1e-05
        PATCH_DIM = C * P * P
        HP = IMG // P

        def layernorm(x, gamma, beta):
            mu = jnp.mean(x, axis=-1, keepdims=True)
            var = jnp.var(x, axis=-1, keepdims=True)
            return (x - mu) * jax.lax.rsqrt(var + EPS) * gamma + beta

        def posemb_sincos_2d(h, w, dim, dtype):
            y, x = jnp.meshgrid(jnp.arange(h), jnp.arange(w), indexing='ij')
            omega = jnp.arange(dim // 4, dtype=jnp.float32) / (dim // 4 - 1)
            omega = 1.0 / TEMP ** omega
            y = y.reshape(-1)[:, None] * omega[None, :]
            x = x.reshape(-1)[:, None] * omega[None, :]
            pe = jnp.concatenate((jnp.sin(x), jnp.cos(x), jnp.sin(y), jnp.cos(y)), axis=1)
            return pe.astype(dtype)
        key = jax.random.key(seed)
        ks = jax.random.split(key, 8)
        B = 64
        img = jax.random.normal(ks[0], (B, C, IMG, IMG), dtype=jnp.float32)
        cls_token = jax.random.normal(ks[1], (1, 1, DIM), dtype=jnp.float32)
        cls_pos_embedding = jax.random.normal(ks[2], (1, 1, DIM), dtype=jnp.float32)
        ln1_g = jnp.ones((PATCH_DIM,), jnp.float32)
        ln1_b = jnp.zeros((PATCH_DIM,), jnp.float32)
        W = jax.random.normal(ks[3], (PATCH_DIM, DIM), dtype=jnp.float32) / np.sqrt(PATCH_DIM)
        bias = jnp.zeros((DIM,), jnp.float32)
        ln2_g = jnp.ones((DIM,), jnp.float32)
        ln2_b = jnp.zeros((DIM,), jnp.float32)
        return {'img': img, 'cls_token': cls_token, 'cls_pos_embedding': cls_pos_embedding, 'ln1_g': ln1_g, 'ln1_b': ln1_b, 'W': W, 'bias': bias, 'ln2_g': ln2_g, 'ln2_b': ln2_b}
    _L0_tok_all = _L0_tok_setup()
    _L0_tok_in = {k: v for k, v in _L0_tok_all.items() if k in ('cls_token', 'cls_pos_embedding', 'ln1_g', 'ln1_b', 'W', 'bias', 'ln2_g', 'ln2_b')}
    del _L0_tok_all

    def _L0_attn_setup():
        import jax, jax.numpy as jnp
        import numpy as np
        B, S, DM, H = (4, 256, 256, 16)
        D = DM // H

        def _split_heads(x):
            return x.reshape(x.shape[0], x.shape[1], H, D).transpose(0, 2, 1, 3)
        key = jax.random.key(seed)
        ks = jax.random.split(key, 16)
        sc = 0.02
        return {'hidden_states': jax.random.normal(ks[0], (B, S, DM), jnp.float32), 'wq': jax.random.normal(ks[1], (DM, DM), jnp.float32) * sc, 'bq': jax.random.normal(ks[2], (DM,), jnp.float32) * sc, 'wk': jax.random.normal(ks[3], (DM, DM), jnp.float32) * sc, 'bk': jax.random.normal(ks[4], (DM,), jnp.float32) * sc, 'wv': jax.random.normal(ks[5], (DM, DM), jnp.float32) * sc, 'bv': jax.random.normal(ks[6], (DM,), jnp.float32) * sc, 'wo': jax.random.normal(ks[7], (DM, DM), jnp.float32) * sc, 'bo': jax.random.normal(ks[8], (DM,), jnp.float32) * sc, 'wfq': jax.random.normal(ks[9], (DM, DM), jnp.float32) * sc, 'bfq': jax.random.normal(ks[10], (DM,), jnp.float32) * sc, 'wfg': jax.random.normal(ks[11], (DM, DM), jnp.float32) * sc, 'bfg': jax.random.normal(ks[12], (DM,), jnp.float32) * sc, 'up': jax.random.normal(ks[13], (H, 1, D), jnp.float32) * sc, 'uz': jax.random.normal(ks[14], (H, 1, D), jnp.float32) * sc}
    _L0_attn_all = _L0_attn_setup()
    _L0_attn_in = {k: v for k, v in _L0_attn_all.items() if k in ('wq', 'bq', 'wk', 'bk', 'wv', 'bv', 'wo', 'bo', 'wfq', 'bfq', 'wfg', 'bfg', 'up', 'uz')}
    del _L0_attn_all

    def _L0_ffn_setup():
        import jax, jax.numpy as jnp
        import numpy as np
        B, S, D, E, H, O = (4, 512, 256, 8, 512, 256)
        key = jax.random.key(seed)
        ks = jax.random.split(key, 8)
        sd = 1.0 / np.sqrt(D)
        sh = 1.0 / np.sqrt(H)
        return {'x': jax.random.normal(ks[0], (B, S, D), dtype=jnp.float32), 'gate_w': jax.random.uniform(ks[1], (D, E), jnp.float32, -sd, sd), 'gate_b': jax.random.uniform(ks[2], (E,), jnp.float32, -sd, sd), 'expert_w': jax.random.uniform(ks[3], (E, D, H), jnp.float32, -sd, sd), 'expert_b': jax.random.uniform(ks[4], (E, H), jnp.float32, -sd, sd), 'out_w': jax.random.uniform(ks[5], (H, O), jnp.float32, -sh, sh), 'out_b': jax.random.uniform(ks[6], (O,), jnp.float32, -sh, sh)}
    _L0_ffn_all = _L0_ffn_setup()
    _L0_ffn_in = {k: v for k, v in _L0_ffn_all.items() if k in ('gate_w', 'gate_b', 'expert_w', 'expert_b', 'out_w', 'out_b')}
    del _L0_ffn_all
    return {'x': x, 'cls_tok': cls_tok, 'L0_tok_cls_token': _L0_tok_in['cls_token'], 'L0_tok_cls_pos_embedding': _L0_tok_in['cls_pos_embedding'], 'L0_tok_ln1_g': _L0_tok_in['ln1_g'], 'L0_tok_ln1_b': _L0_tok_in['ln1_b'], 'L0_tok_W': _L0_tok_in['W'], 'L0_tok_bias': _L0_tok_in['bias'], 'L0_tok_ln2_g': _L0_tok_in['ln2_g'], 'L0_tok_ln2_b': _L0_tok_in['ln2_b'], 'L0_attn_wq': _L0_attn_in['wq'], 'L0_attn_bq': _L0_attn_in['bq'], 'L0_attn_wk': _L0_attn_in['wk'], 'L0_attn_bk': _L0_attn_in['bk'], 'L0_attn_wv': _L0_attn_in['wv'], 'L0_attn_bv': _L0_attn_in['bv'], 'L0_attn_wo': _L0_attn_in['wo'], 'L0_attn_bo': _L0_attn_in['bo'], 'L0_attn_wfq': _L0_attn_in['wfq'], 'L0_attn_bfq': _L0_attn_in['bfq'], 'L0_attn_wfg': _L0_attn_in['wfg'], 'L0_attn_bfg': _L0_attn_in['bfg'], 'L0_attn_up': _L0_attn_in['up'], 'L0_attn_uz': _L0_attn_in['uz'], 'L0_ffn_gate_w': _L0_ffn_in['gate_w'], 'L0_ffn_gate_b': _L0_ffn_in['gate_b'], 'L0_ffn_expert_w': _L0_ffn_in['expert_w'], 'L0_ffn_expert_b': _L0_ffn_in['expert_b'], 'L0_ffn_out_w': _L0_ffn_in['out_w'], 'L0_ffn_out_b': _L0_ffn_in['out_b']}

def reference(x, cls_tok, L0_tok_cls_token, L0_tok_cls_pos_embedding, L0_tok_ln1_g, L0_tok_ln1_b, L0_tok_W, L0_tok_bias, L0_tok_ln2_g, L0_tok_ln2_b, L0_attn_wq, L0_attn_bq, L0_attn_wk, L0_attn_bk, L0_attn_wv, L0_attn_bv, L0_attn_wo, L0_attn_bo, L0_attn_wfq, L0_attn_bfq, L0_attn_wfg, L0_attn_bfg, L0_attn_up, L0_attn_uz, L0_ffn_gate_w, L0_ffn_gate_b, L0_ffn_expert_w, L0_ffn_expert_b, L0_ffn_out_w, L0_ffn_out_b):
    import jax
    import jax.numpy as jnp

    def _L0_tok_ref(img, cls_token, cls_pos_embedding, ln1_g, ln1_b, W, bias, ln2_g, ln2_b):
        import jax, jax.numpy as jnp
        import numpy as np
        DIM = 256
        IMG = 96
        P = 16
        C = 3
        TEMP = 10000.0
        EPS = 1e-05
        PATCH_DIM = C * P * P
        HP = IMG // P

        def layernorm(x, gamma, beta):
            mu = jnp.mean(x, axis=-1, keepdims=True)
            var = jnp.var(x, axis=-1, keepdims=True)
            return (x - mu) * jax.lax.rsqrt(var + EPS) * gamma + beta

        def posemb_sincos_2d(h, w, dim, dtype):
            y, x = jnp.meshgrid(jnp.arange(h), jnp.arange(w), indexing='ij')
            omega = jnp.arange(dim // 4, dtype=jnp.float32) / (dim // 4 - 1)
            omega = 1.0 / TEMP ** omega
            y = y.reshape(-1)[:, None] * omega[None, :]
            x = x.reshape(-1)[:, None] * omega[None, :]
            pe = jnp.concatenate((jnp.sin(x), jnp.cos(x), jnp.sin(y), jnp.cos(y)), axis=1)
            return pe.astype(dtype)
        b = img.shape[0]
        x = img.reshape(b, C, HP, P, HP, P)
        x = jnp.transpose(x, (0, 2, 4, 3, 5, 1))
        x = x.reshape(b, HP, HP, PATCH_DIM)
        x = layernorm(x, ln1_g, ln1_b)
        x = jnp.einsum('bhwp,pd->bhwd', x, W) + bias
        x = layernorm(x, ln2_g, ln2_b)
        pe = posemb_sincos_2d(HP, HP, DIM, x.dtype)
        x = x.reshape(b, HP * HP, DIM) + pe[None]
        cls_tokens = jnp.broadcast_to(cls_token + cls_pos_embedding, (b, 1, DIM))
        return jnp.concatenate((cls_tokens, x), axis=1)

    def _L0_attn_ref(hidden_states, wq, bq, wk, bk, wv, bv, wo, bo, wfq, bfq, wfg, bfg, up, uz):
        import jax, jax.numpy as jnp
        import numpy as np
        B, S, DM, H = (4, 256, 256, 16)
        D = DM // H

        def _split_heads(x):
            return x.reshape(x.shape[0], x.shape[1], H, D).transpose(0, 2, 1, 3)
        key_len = hidden_states.shape[1]
        mixed_q = hidden_states @ wq + bq
        mixed_k = hidden_states @ wk + bk
        mixed_v = hidden_states @ wv + bv
        glo = jnp.mean(mixed_q, axis=1, keepdims=True)
        c = jnp.tanh(mixed_q @ wfq + bfq + (glo @ wfg + bfg))
        c = _split_heads(c)
        p = jnp.sum(c * up[None], axis=-1)
        z = jnp.sum(c * uz[None], axis=-1)
        P = jax.nn.sigmoid(p) * key_len
        Z = jax.nn.sigmoid(z) * key_len
        j = jnp.arange(key_len, dtype=P.dtype)
        G = -(j[None, None, None, :] - P[..., None]) ** 2 * 2.0 / Z[..., None] ** 2
        q = _split_heads(mixed_q)
        k = _split_heads(mixed_k)
        v = _split_heads(mixed_v)
        scores = jnp.einsum('bhqd,bhkd->bhqk', q, k) / jnp.sqrt(jnp.float32(D))
        scores = scores + G
        probs = jax.nn.softmax(scores, axis=-1)
        ctx = jnp.einsum('bhqk,bhkd->bhqd', probs, v)
        ctx = ctx.transpose(0, 2, 1, 3).reshape(ctx.shape[0], key_len, H * D)
        return ctx @ wo + bo

    def _L0_ffn_ref(x, gate_w, gate_b, expert_w, expert_b, out_w, out_b):
        import jax, jax.numpy as jnp
        import numpy as np
        B, S, D, E, H, O = (4, 512, 256, 8, 512, 256)
        Bq, Sq, Dq = x.shape
        xt = x.reshape(-1, Dq)
        logits = xt @ gate_w + gate_b
        idx = jnp.argmax(logits, axis=-1)
        all_out = jnp.einsum('td,edh->teh', xt, expert_w) + expert_b[None]
        onehot = jax.nn.one_hot(idx, expert_w.shape[0], dtype=x.dtype)
        sel = jnp.einsum('te,teh->th', onehot, all_out)
        out = sel @ out_w + out_b
        return out.reshape(Bq, Sq, -1)
    h = _L0_tok_ref(x, L0_tok_cls_token, L0_tok_cls_pos_embedding, L0_tok_ln1_g, L0_tok_ln1_b, L0_tok_W, L0_tok_bias, L0_tok_ln2_g, L0_tok_ln2_b)
    h = jnp.concatenate([jnp.broadcast_to(cls_tok, (h.shape[0], 1, h.shape[2])), h], axis=1)
    h = h + _L0_attn_ref(_layernorm(h, axis=-1), L0_attn_wq, L0_attn_bq, L0_attn_wk, L0_attn_bk, L0_attn_wv, L0_attn_bv, L0_attn_wo, L0_attn_bo, L0_attn_wfq, L0_attn_bfq, L0_attn_wfg, L0_attn_bfg, L0_attn_up, L0_attn_uz)
    h = h + _L0_ffn_ref(_layernorm(h, axis=-1), L0_ffn_gate_w, L0_ffn_gate_b, L0_ffn_expert_w, L0_ffn_expert_b, L0_ffn_out_w, L0_ffn_out_b)
    return h

_drawn_inputs = setup_inputs


def setup_inputs(seed=0):
    import zlib

    import numpy as np

    out = dict(_drawn_inputs(seed))
    spreads = {'L0_tok_ln1_g': (1.0, 0.2),
     'L0_tok_ln1_b': (0.0, 0.1),
     'L0_tok_bias': (0.0, 0.1),
     'L0_tok_ln2_g': (1.0, 0.2),
     'L0_tok_ln2_b': (0.0, 0.1)}
    factors = {'cls_tok': 2.68,
     'L0_attn_wq': 7.269,
     'L0_attn_bq': 8.0,
     'L0_attn_wk': 4.309,
     'L0_attn_bk': 200.0,
     'L0_attn_wfq': 8.0,
     'L0_attn_bfq': 59.738,
     'L0_attn_wfg': 8.0,
     'L0_attn_bfg': 108.588,
     'L0_attn_up': 8.0,
     'L0_attn_uz': 8.0,
     'L0_ffn_expert_b': 3.456,
     'L0_ffn_out_b': 2.788}
    for name, (base, spread) in spreads.items():
        noise = np.random.default_rng([zlib.crc32(name.encode()), seed]).standard_normal(out[name].shape)
        drawn = base * np.exp(spread * noise) if base else spread * noise
        out[name] = jnp.asarray(drawn.astype(out[name].dtype))
    for name, factor in factors.items():
        out[name] = (out[name] * factor).astype(out[name].dtype)
    return out
```

```python
import numpy as np
import concourse.bass as bass
from concourse import mybir
from concourse.alu_op_type import AluOpType as ALU
from contextlib import ExitStack

F32 = mybir.dt.float32
F32R = mybir.dt.float32r
U32 = mybir.dt.uint32
ACT = mybir.ActivationFunctionType
AX = mybir.AxisListType

BATCH, CH, IMG, PATCH = 32, 3, 96, 16
GRID = IMG // PATCH
DIM = 256
PDIM = CH * PATCH * PATCH
KC = DIM // 128
PC = PDIM // 128
SEQ = GRID * GRID + 2
HEADS, HD = 16, 16
HH = HEADS // 2
EXPERTS, HID = 8, 512
HC = HID // 128
IMGS = 3
TOK = IMGS * SEQ
TILES = -(-BATCH // IMGS)
EPS = 1e-5
PAIR = 2 * SEQ
HALF = HH * SEQ
ROOT2 = float(np.sqrt(2.0))

C_ID, C_PE, C_J, C_MASK, C_IOTA, C_SEL = 0, 128, 384, 992, 993, 1001
C_END = C_SEL + TOK
L_G1, L_B1, L_BQ, L_BK, L_BFQ, L_BFG, L_BV = 0, 6, 12, 14, 16, 18, 20
L_UPZ, L_GATE, L_EB = 22, 86, 102
L_END = L_EB + HC * EXPERTS
R_BIAS, R_G2, R_BO, R_OB, R_GB = 0, 256, 512, 768, 1024
R_END = 1032


def vit_tower(nc, x, w_patch, w_attn, w_exp, w_out, consts, cols, rows, heads4, out):
    es = ExitStack()
    with es:
        def sb(name, shape, dt=F32):
            return es.enter_context(nc.sbuf_tensor(name, shape, dt))

        def sem(name):
            return es.enter_context(nc.semaphore(name))

        cst = sb("cst", [128, C_END])
        col = sb("col", [128, L_END])
        row = sb("row", [TOK, R_END])
        head4 = sb("head4", [4, DIM])
        wp = sb("wp", [128, PC, DIM])
        wp_hi = sb("wp_hi", [128, PC, DIM], F32R)
        wp_lo = sb("wp_lo", [128, PC, DIM], F32R)
        wa = sb("wa", [128, 6, KC, DIM])
        wa_hi = sb("wa_hi", [128, 5, KC, DIM], F32R)
        wa_lo = sb("wa_lo", [128, 5, KC, DIM], F32R)
        WQ, WK, WV, WFQ, WO, WFG = range(6)
        gate_hi = sb("gate_hi", [128, KC, EXPERTS], F32R)
        gate_lo = sb("gate_lo", [128, KC, EXPERTS], F32R)
        wexp = sb("wexp", [128, HC, 4, DIM])
        wout = sb("wout", [128, HC, DIM])
        fold_hi = sb("fold_hi", [128, EXPERTS, KC, DIM], F32R)
        fold_lo = sb("fold_lo", [128, EXPERTS, KC, DIM], F32R)
        fold_bias = sb("fold_bias", [EXPERTS, DIM])
        jmat = sb("jmat", [4 * HEADS, HEADS * SEQ], F32R)
        bias1 = sb("bias1", [TOK, DIM])
        extra = sb("extra", [TOK, DIM])
        bias_o = sb("bias_o", [TOK, DIM])
        nhalf = sb("nhalf", [TOK, 1])
        bk4 = sb("bk4", [128, KC])
        bf = sb("bf", [128, KC])
        xt = sb("xt", [TOK, PDIM])
        xn = sb("xn", [TOK, PDIM])
        st1 = sb("st1", [TOK, 2, 6])
        mv1 = sb("mv1", [TOK, 2])
        ve1 = sb("ve1", [TOK, 1])
        rs1 = sb("rs1", [TOK, 1])
        xT_hi = sb("xT_hi", [128, PC, TOK], F32R)
        xT_lo = sb("xT_lo", [128, PC, TOK], F32R)
        y = sb("y", [TOK, DIM])
        st2 = sb("st2", [TOK, 6])
        mv2 = sb("mv2", [TOK, 2])
        ve2 = sb("ve2", [TOK, 1])
        rs2 = sb("rs2", [TOK, 1])
        rs2m = sb("rs2m", [TOK, 1])
        yg = sb("yg", [TOK, DIM])
        h = sb("h", [TOK, DIM])
        h_res = sb("h_res", [TOK, TILES, DIM])
        st3 = sb("st3", [TOK, 6])
        mv3 = sb("mv3", [TOK, 2])
        ve3 = sb("ve3", [TOK, 1])
        rs3 = sb("rs3", [TOK, 1])
        hn = sb("hn", [TOK, DIM])
        hT_hi = sb("hT_hi", [128, KC, TOK], F32R)
        hT_lo = sb("hT_lo", [128, KC, TOK], F32R)
        q = sb("q", [128, KC, TOK])
        q_hi = sb("q_hi", [128, KC, IMGS, TOK], F32R)
        q_lo = sb("q_lo", [128, KC, IMGS, TOK], F32R)
        k = sb("k", [128, KC, TOK])
        k_s = sb("k_s", [128, 2, KC, TOK], F32R)
        k_bd = sb("k_bd", [128, 2 * KC, HH, TOK], F32R)
        v_s = sb("v_s", [TOK, 2, HH, 2, HD])
        v_bd = sb("v_bd", [PAIR, IMGS, DIM])
        gsum = sb("gsum", [128, KC * IMGS])
        glo = sb("glo", [128, KC * IMGS])
        gbias = sb("gbias", [128, KC, IMGS])
        cpre = sb("cpre", [128, KC, TOK])
        cth = sb("cth", [128, KC, TOK])
        epz = sb("epz", [TOK, 2 * HEADS])
        epz1 = sb("epz1", [TOK, 2 * HEADS])
        rp = sb("rp", [TOK, HEADS])
        sp = sb("sp", [TOK, 2 * HEADS])
        sp4 = sb("sp4", [TOK, 4 * HEADS])
        sp4r = sb("sp4r", [TOK, 2 * HEADS], F32R)
        spT = sb("spT", [4 * HEADS, TOK], F32R)
        sq = sb("sq", [TOK, HEADS, SEQ])
        sc = sb("sc", [TOK, HEADS, SEQ])
        smax = sb("smax", [TOK, HEADS])
        sd = sb("sd", [TOK, HEADS, SEQ])
        ex = sb("ex", [TOK, HEADS, SEQ])
        ssum = sb("ssum", [TOK, HEADS])
        rsum = sb("rsum", [TOK, HEADS])
        pr = sb("pr", [TOK, HEADS, SEQ])
        pT = sb("pT", [PAIR, HH, TOK])
        ctx_hi = sb("ctx_hi", [128, KC, TOK], F32R)
        ctx_lo = sb("ctx_lo", [128, KC, TOK], F32R)
        h2 = sb("h2", [TOK, DIM])
        st4 = sb("st4", [TOK, 6])
        mv4 = sb("mv4", [TOK, 2])
        ve4 = sb("ve4", [TOK, 1])
        rs4 = sb("rs4", [TOK, 1])
        un = sb("un", [TOK, DIM])
        uT_hi = sb("uT_hi", [128, KC, TOK], F32R)
        uT_lo = sb("uT_lo", [128, KC, TOK], F32R)
        logit = sb("logit", [TOK, EXPERTS])
        top = sb("top", [TOK, 8])
        topi = sb("topi", [TOK, 8], U32)
        topf = sb("topf", [TOK, 1])
        hot = sb("hot", [TOK, EXPERTS])
        hotT = sb("hotT", [EXPERTS, TOK])
        acc = sb("acc", [TOK, 2, DIM])
        res = sb("res", [TOK, DIM])

        bank = [es.enter_context(nc.psum_tensor(f"bank{i}", [128, 512], F32)) for i in range(8)]

        ident = cst[:, C_ID:C_ID + 128]
        idtok = cst[0:TOK, C_ID:C_ID + TOK]
        pe_pos = cst[0:TOK, C_PE:C_PE + DIM]
        patch_mask = cst[0:TOK, C_MASK:C_MASK + 1]
        iota8 = cst[0:TOK, C_IOTA:C_IOTA + EXPERTS]
        sel4 = cst[0:4, C_SEL:C_SEL + TOK]
        upz = col[:, L_UPZ:L_UPZ + KC * 2 * HEADS].rearrange("p (k n) -> p k n", k=KC)
        gate = col[:, L_GATE:L_GATE + KC * EXPERTS].rearrange("p (k n) -> p k n", k=KC)
        ebT = col[:, L_EB:L_EB + HC * EXPERTS].rearrange("p (k n) -> p k n", k=HC)

        done = {name: sem("s_" + name) for name in """ld_cst ld_col ld_row ld_head4 ld_wp ld_wa ld_wout
            zeros nhalf bias_cols wp_hi wp_lo wa_hi wa_lo gate_hi gate_lo jmat
            mm_bias1 mm_bias_o mm_extra mm_fb bias1 bias_o extra fold_bias
            mm_fold fold_hi fold_lo
            ld_x st1 mv1 ve1 rs1 xn mm_xT xT_hi xT_lo mm_y y st2 mv2 ve2 rs2 rs2m yg h h_res
            st3 mv3 ve3 rs3 hn mm_hT hT_hi hT_lo mm_q q q_hi q_lo mm_k k k_hi k_lo k_bd
            mm_v v_s v_bd gsum glo mm_c gbias cpre cth mm_pz epz epz1 rp sps spn sp sp_hi sp_hic sp_lo mm_spT spT
            mm_g mm_s sq sc smax sd ex ssum rsum pr mm_pT pT mm_ctx ctx_hi ctx_lo mm_o h2
            st4 mv4 ve4 rs4 un mm_uT uT_hi uT_lo mm_lg logit top topi topf hot mm_f acc
            mm_hotT hotT mm_fbias res stored""".split()}

        ld_wexp = [sem(f"s_ld_wexp{n}") for n in range(2)]

        block = es.enter_context(nc.Block())

        def free(eng, semaphore, n):
            if not (isinstance(n, int) and n <= 0):
                eng.wait_ge(semaphore, n)

        def wait_apart(eng, semaphore, n, settled):
            if not isinstance(n, int):
                eng.wait_ge(settled, 1)
            eng.wait_ge(semaphore, n)

        def run(eng, iteration):
            iteration(0, True, False, False)
            iteration(1, True, True, False)
            iteration(2, True, True, True)
            with eng.Fori(3, TILES - 1) as i:
                iteration(i, True, True, True)
            iteration(TILES - 1, True, True, True)
            iteration(TILES, False, True, True)
            iteration(TILES + 1, False, False, True)

        @block.sync
        def _(sync):
            sync.dma_start(xt[:], x[0:TOK, :]).then_inc(done["ld_x"], 16)
            sync.dma_start(wp[:], w_patch).then_inc(done["ld_wp"], 16)
            sync.dma_start(wa[:], w_attn).then_inc(done["ld_wa"], 16)

            def load_experts(n):
                if n >= 2:
                    sync.wait_ge(done["mm_fold"], 2 * n - 2)
                at = 2 * (n % 2)
                sync.dma_start(wexp[:, :, at:at + 2, :], w_exp[:, :, 2 * n:2 * n + 2, :]).then_inc(ld_wexp[n % 2], 16)

            load_experts(0)
            load_experts(1)

            def iteration(i, a, b, c):
                if a:
                    if not (isinstance(i, int) and i == TILES - 1):
                        sync.wait_ge(done["xn"], i + 1)
                        sync.dma_start(xt[:], x[bass.ds((i + 1) * TOK, TOK), :]).then_inc(done["ld_x"], 16)
                    if isinstance(i, int) and i == 0:
                        load_experts(2)
                        load_experts(3)
                    sync.wait_ge(done["k_lo"], i + 1)
                    free(sync, done["mm_s"], i)
                    sync.wait_ge(done["zeros"], 4)
                    for hd in range(HH):
                        part = slice(hd * HD, (hd + 1) * HD)
                        sync.dma_start(
                            k_bd[part, :, hd, :].bitcast(F32),
                            k_s[part].rearrange("p a k t -> p (a k) t").bitcast(F32)).then_inc(done["k_bd"], 16)
                if c:
                    sync.wait_ge(done["res"], i - 1)
                    sync.dma_start(out[bass.ds((i - 2) * TOK, TOK), :], res[:]).then_inc(done["stored"], 16)

            run(sync, iteration)
            sync.wait_ge(done["stored"], 16 * TILES)

        @block.gpsimd
        def _(pool):
            pool.dma_start(cst[:], consts).then_inc(done["ld_cst"], 16)
            pool.memset(nhalf[:], -0.5).then_inc(done["nhalf"], 1)
            pool.memset(q_hi[:].bitcast(F32), 0.0).then_inc(done["zeros"], 1)
            pool.memset(q_lo[:].bitcast(F32), 0.0).then_inc(done["zeros"], 1)
            pool.memset(v_s[:], 0.0).then_inc(done["zeros"], 1)
            pool.memset(k_bd[:].bitcast(F32), 0.0).then_inc(done["zeros"], 1)
            pool.wait_ge(done["nhalf"], 1)

            def rstd(out_ap, in_ap, ready, result, n):
                pool.wait_ge(ready, n)
                pool.tensor_tensor(out_ap, in_ap, nhalf[:], ALU.pow).then_inc(result, 1)

            rstd(rs1[:], ve1[:], done["ve1"], done["rs1"], 1)

            def iteration(i, a, b, c):
                if c:
                    rstd(rs4[:], ve4[:], done["ve4"], done["rs4"], i - 1)
                if b:
                    pool.wait_ge(done["smax"], i)
                    pool.tensor_tensor(sd[:], sc[:], smax[:].unsqueeze(2).to_broadcast([TOK, HEADS, SEQ]),
                                       ALU.subtract).then_inc(done["sd"], 1)
                if a:
                    rstd(rs2[:], ve2[:], done["ve2"], done["rs2"], i + 1)
                    rstd(rs3[:], ve3[:], done["ve3"], done["rs3"], i + 1)
                if b:
                    pool.wait_ge(done["rsum"], i)
                    pool.tensor_tensor(pr[:], ex[:], rsum[:].unsqueeze(2).to_broadcast([TOK, HEADS, SEQ]),
                                       ALU.mult).then_inc(done["pr"], 1)
                if a:
                    if isinstance(i, int) and i == 0:
                        pool.wait_ge(done["bias_o"], 1)
                    pool.tensor_tensor(h_res[:, bass.ds(i, 1), :].rearrange("p a d -> p (a d)"), h[:], bias_o[:],
                                       ALU.add).then_inc(done["h_res"], 1)
                    pool.wait_ge(done["q_hi"], i + 1)
                    for kc in range(KC):
                        o = q_lo[:, kc].rearrange("p g t -> p (g t)")
                        hi = q_hi[:, kc].bitcast(F32).rearrange("p g t -> p (g t)")
                        for g in range(IMGS):
                            d = slice(g * (TOK + SEQ), g * (TOK + SEQ) + SEQ)
                            pool.tensor_tensor(o[:, d], q[:, kc, g * SEQ:(g + 1) * SEQ], hi[:, d],
                                               ALU.subtract).then_inc(done["q_lo"], 1)
                    pool.wait_ge(done["nhalf"], 1)
                    free(pool, done["mm_ctx"], i)
                    pool.wait_ge(done["v_s"], i + 1)
                    for g in range(IMGS):
                        for par in range(2):
                            pool.dma_start(v_bd[par * SEQ:(par + 1) * SEQ, g, :],
                                           v_s[g * SEQ:(g + 1) * SEQ, par].rearrange("p a b d -> p (a b d)"))\
                                .then_inc(done["v_bd"], 16)
                    if not (isinstance(i, int) and i == TILES - 1):
                        rstd(rs1[:], ve1[:], done["ve1"], done["rs1"], i + 2)

            run(pool, iteration)

        @block.scalar
        def _(act):
            act.dma_start(col[:], cols).then_inc(done["ld_col"], 16)
            act.dma_start(row[:], rows.to_broadcast([TOK, R_END])).then_inc(done["ld_row"], 16)
            act.dma_start(head4[:], heads4).then_inc(done["ld_head4"], 16)
            act.dma_start(wout[:], w_out).then_inc(done["ld_wout"], 16)

            act.wait_ge(done["ld_col"], 16)
            act.wait_ge(done["ld_wp"], 16)
            for j in range(PC):
                act.activation(wp_hi[:, j, :], wp[:, j, :], ACT.Copy,
                               scale=col[:, L_G1 + j:L_G1 + j + 1]).then_inc(done["wp_hi"], 1)
            act.wait_ge(done["ld_wa"], 16)
            for j in range(5):
                act.copy(wa_hi[:, j], wa[:, j]).then_inc(done["wa_hi"], 1)
            act.copy(gate_hi[:], gate).then_inc(done["gate_hi"], 1)
            act.wait_ge(done["ld_cst"], 16)
            act.copy(jmat[:], cst[0:4 * HEADS, C_J:C_J + HEADS * SEQ]).then_inc(done["jmat"], 1)

            def fold_hi_part(e0, e1):
                for e in range(e0, e1):
                    act.wait_ge(done["mm_fold"], e + 1)
                    act.copy(fold_hi[:, e].rearrange("p k d -> p (k d)"), bank[2 + e % 2][:, :]).then_inc(done["fold_hi"], 1)

            def iteration(i, a, b, c):
                if a:
                    for n in range(2):
                        act.wait_ge(done["mm_xT"], 2 * i + n + 1)
                        if n == 0:
                            free(act, done["mm_y"], i)
                        act.copy(xT_hi[:, 3 * n:3 * n + 3, :].rearrange("p c t -> p (c t)"),
                                 bank[n][:, 0:3 * TOK]).then_inc(done["xT_hi"], 1)
                if b:
                    for n in range(2):
                        act.wait_ge(done["mm_g"], 2 * (i - 1) + n + 1)
                        if n == 0:
                            free(act, done["sc"], 2 * (i - 1))
                        act.activation(sq[:, n * HH:(n + 1) * HH, :].rearrange("p a b -> p (a b)"),
                                       bank[6 + n][0:TOK, 0:HALF], ACT.Square).then_inc(done["sq"], 1)
                if c:
                    act.wait_ge(done["mm_uT"], i - 1)
                    free(act, done["mm_f"], 4 * (i - 2))
                    act.copy(uT_hi[:].rearrange("p c t -> p (c t)"), bank[2][:, 0:KC * TOK]).then_inc(done["uT_hi"], 1)
                if b:
                    act.wait_ge(done["sd"], i)
                    free(act, done["pr"], i - 1)
                    act.activation(ex[:], sd[:], ACT.Exp).then_inc(done["ex"], 1)
                if isinstance(i, int) and i < 2:
                    fold_hi_part(4 * i, 4 * i + 4)
                if a:
                    act.wait_ge(done["mm_hT"], i + 1)
                    free(act, done["mm_v"], i)
                    act.copy(hT_hi[:].rearrange("p c t -> p (c t)"), bank[1][:, 0:KC * TOK]).then_inc(done["hT_hi"], 1)
                if b:
                    act.wait_ge(done["mm_pT"], 2 * (i - 1) + 1)
                    free(act, done["mm_ctx"], i - 1)
                    act.copy(pT[:, 0:HH // 2, :].rearrange("p c t -> p (c t)"),
                             bank[6][0:PAIR, 0:HH // 2 * TOK]).then_inc(done["pT"], 1)
                if a:
                    act.wait_ge(done["mm_q"], i + 1)
                    free(act, done["q_lo"], KC * IMGS * i)
                    free(act, done["gsum"], i)
                    for m in range(KC):
                        act.activation(q[:, m, :], bank[0][:, m * TOK:(m + 1) * TOK], ACT.Identity,
                                       bias=col[:, L_BQ + m:L_BQ + m + 1]).then_inc(done["q"], 1)
                    act.wait_ge(done["q"], KC * (i + 1))
                    if isinstance(i, int) and i == 0:
                        act.wait_ge(done["zeros"], 4)
                    for m in range(KC):
                        flat = q_hi[:, m].rearrange("p g t -> p (g t)")
                        for g in range(IMGS):
                            ins = act.copy(flat[:, g * (TOK + SEQ):g * (TOK + SEQ) + SEQ],
                                           q[:, m, g * SEQ:(g + 1) * SEQ])
                    ins.then_inc(done["q_hi"], 1)
                if b:
                    act.wait_ge(done["mm_ctx"], i)
                    free(act, done["mm_o"], i - 1)
                    act.copy(ctx_hi[:].rearrange("p c t -> p (c t)"), bank[4][:, 0:KC * TOK]).then_inc(done["ctx_hi"], 1)
                if a:
                    act.wait_ge(done["mm_v"], i + 1)
                    free(act, done["v_bd"], 6 * 16 * i)
                    pv = bank[0][0:TOK, 0:DIM].rearrange("p (a b d) -> p a b d", a=HH, b=2)
                    for par in range(2):
                        ins = act.copy(v_s[:, par, :, par, :], pv[:, :, par, :])
                    ins.then_inc(done["v_s"], 1)
                    act.wait_ge(done["cpre"], i + 1)
                    free(act, done["mm_pz"], i)
                    act.activation(cth[:], cpre[:], ACT.Tanh).then_inc(done["cth"], 1)
                    act.wait_ge(done["mm_pz"], i + 1)
                    act.activation(epz[:], bank[0][0:TOK, 0:2 * HEADS], ACT.Exp, scale=-1.0).then_inc(done["epz"], 1)

            run(act, iteration)

        @block.tensor
        def _(pe):
            def mm3(o, left, right):
                last = len(left) - 1
                for n, ((lh, ll), (rh, rl)) in enumerate(zip(left, right)):
                    pe.matmul(o, lh, rh, start=(n == 0), stop=False)
                    pe.matmul(o, lh, rl, start=False, stop=False)
                    ins = pe.matmul(o, ll, rh, start=False, stop=(n == last))
                return ins

            pe.wait_ge(done["ld_col"], 16)
            pe.wait_ge(done["ld_wp"], 16)
            for j in range(PC):
                ins = pe.matmul(bank[4][0:TOK, 0:DIM], col[:, L_B1 + j:L_B1 + j + 1].to_broadcast([128, TOK]),
                                wp[:, j, :], start=(j == 0), stop=(j == PC - 1))
            ins.then_inc(done["mm_bias1"], 1)
            pe.wait_ge(done["ld_cst"], 16)
            pe.wait_ge(done["ld_head4"], 16)
            pe.matmul(bank[6][0:TOK, 0:DIM], sel4, head4[:], start=True, stop=True).then_inc(done["mm_extra"], 1)
            pe.wait_ge(done["ld_wa"], 16)
            for j in range(KC):
                ins = pe.matmul(bank[5][0:TOK, 0:DIM], col[:, L_BV + j:L_BV + j + 1].to_broadcast([128, TOK]),
                                wa[:, WO, j, :], start=(j == 0), stop=(j == KC - 1))
            ins.then_inc(done["mm_bias_o"], 1)
            pe.wait_ge(done["ld_wout"], 16)
            for j in range(HC):
                ins = pe.matmul(bank[7][0:EXPERTS, 0:DIM], ebT[:, j, :], wout[:, j, :],
                                start=(j == 0), stop=(j == HC - 1))
            ins.then_inc(done["mm_fb"], 1)

            def fold(e0, e1):
                for e in range(e0, e1):
                    pe.wait_ge(ld_wexp[e // 2 % 2], 16 * (e // 4 + 1))
                    if e >= 2:
                        pe.wait_ge(done["fold_lo"], e - 1)
                    for m in range(KC):
                        for j in range(HC):
                            ins = pe.matmul(bank[2 + e % 2][:, m * DIM:(m + 1) * DIM],
                                            wexp[:, j, e % 4, m * 128:(m + 1) * 128], wout[:, j, :],
                                            start=(j == 0), stop=(j == HC - 1))
                    ins.then_inc(done["mm_fold"], 1)

            def iteration(i, a, b, c):
                first = isinstance(i, int) and i == 0
                if a:
                    pe.wait_ge(done["xn"], i + 1)
                    free(pe, done["epz"], i)
                    for n in range(2):
                        if n == 1:
                            free(pe, done["spT"], i)
                        for j in range(3):
                            ins = pe.transpose(bank[n][:, j * TOK:(j + 1) * TOK],
                                               xn[:, (3 * n + j) * 128:(3 * n + j + 1) * 128], idtok)
                        ins.then_inc(done["mm_xT"], 1)
                if b:
                    pe.wait_ge(done["spT"], i)
                    if isinstance(i, int) and i == 1:
                        pe.wait_ge(done["jmat"], 1)
                        pe.wait_ge(done["extra"], 1)
                        pe.wait_ge(done["fold_bias"], 1)
                    free(pe, done["pT"], 2 * (i - 1))
                    for n in range(2):
                        pe.matmul(bank[6 + n][0:TOK, 0:HALF], spT[:], jmat[:, n * HALF:(n + 1) * HALF],
                                  start=True, stop=True).then_inc(done["mm_g"], 1)
                    pe.wait_ge(done["k_bd"], 16 * HH * i)
                    pe.wait_ge(done["q_lo"], KC * IMGS * i)
                    free(pe, done["ctx_lo"], i - 1)
                    free(pe, done["h2"], i - 1)
                    for n in range(2):
                        o = bank[4 + n][0:TOK, 0:HALF].rearrange("p (a b) -> p a b", a=HH)
                        keys = [tuple(k_bd[:, KC * w + n, :, g * SEQ:(g + 1) * SEQ] for w in range(2))
                                for g in range(IMGS)]
                        mm3(o, [(q_hi[:, n, g, :], q_lo[:, n, g, :]) for g in range(IMGS)],
                            keys).then_inc(done["mm_s"], 1)
                if a:
                    if first:
                        pe.wait_ge(done["wp_lo"], PC)
                    pe.wait_ge(done["xT_lo"], 2 * (i + 1))
                    mm3(bank[0][0:TOK, 0:DIM], [(xT_hi[:, j, :], xT_lo[:, j, :]) for j in range(PC)],
                        [(wp_hi[:, j, :], wp_lo[:, j, :]) for j in range(PC)]).then_inc(done["mm_y"], 1)
                if isinstance(i, int) and i < 2:
                    fold(4 * i, 4 * i + 4)

                def experts(n):
                    for e in (2 * n, 2 * n + 1):
                        ins = mm3(bank[2 + n % 2][0:TOK, (e % 2) * DIM:(e % 2 + 1) * DIM],
                                  [(uT_hi[:, j, :], uT_lo[:, j, :]) for j in range(KC)],
                                  [(fold_hi[:, e, j, :], fold_lo[:, e, j, :]) for j in range(KC)])
                    ins.then_inc(done["mm_f"], 1)

                if c:
                    pe.wait_ge(done["un"], i - 1)
                    free(pe, done["res"], i - 2)
                    if isinstance(i, int) and i == 2:
                        pe.wait_ge(done["fold_lo"], EXPERTS)
                    for j in range(KC):
                        ins = pe.transpose(bank[2][:, j * TOK:(j + 1) * TOK], un[:, j * 128:(j + 1) * 128], idtok)
                    ins.then_inc(done["mm_uT"], 1)
                    pe.wait_ge(done["uT_lo"], i - 1)
                    free(pe, done["acc"], EXPERTS * (i - 2))
                    mm3(bank[3][0:TOK, 0:EXPERTS], [(uT_hi[:, j, :], uT_lo[:, j, :]) for j in range(KC)],
                        [(gate_hi[:, j, :], gate_lo[:, j, :]) for j in range(KC)]).then_inc(done["mm_lg"], 1)
                    experts(0)
                    pe.wait_ge(done["logit"], i - 1)
                    experts(1)
                if a:
                    pe.wait_ge(done["hn"], i + 1)
                    for j in range(KC):
                        ins = pe.transpose(bank[1][:, j * TOK:(j + 1) * TOK], hn[:, j * 128:(j + 1) * 128], idtok)
                    ins.then_inc(done["mm_hT"], 1)
                if b:
                    pe.wait_ge(done["pr"], i)
                    for n in range(2):
                        for j in range(HH // 2):
                            pair = pr[:, (n * HH + 2 * j):(n * HH + 2 * j + 2), :].rearrange("p a b -> p (a b)")
                            ins = pe.transpose(bank[6 + n][0:PAIR, j * TOK:(j + 1) * TOK], pair, idtok)
                        ins.then_inc(done["mm_pT"], 1)
                if c:
                    pe.wait_ge(done["acc"], EXPERTS * (i - 2) + 2)
                    experts(2)
                if a:
                    if first:
                        pe.wait_ge(done["wa_lo"], 5)
                    pe.wait_ge(done["hT_lo"], i + 1)
                    hT = [(hT_hi[:, j, :], hT_lo[:, j, :]) for j in range(KC)]

                    def project(bk, which, moving, result):
                        for m in range(KC):
                            ins = mm3(bank[bk][:, m * TOK:(m + 1) * TOK],
                                      [(wa_hi[:, which, j, m * 128:(m + 1) * 128],
                                        wa_lo[:, which, j, m * 128:(m + 1) * 128]) for j in range(KC)], moving)
                        ins.then_inc(result, 1)

                    project(0, WQ, hT, done["mm_q"])
                    project(1, WK, hT, done["mm_k"])
                if b:
                    pe.wait_ge(done["pT"], 2 * i)
                    pe.wait_ge(done["v_bd"], 6 * 16 * i)
                    pe.wait_ge(done["sc"], 2 * i)
                    for j in range(HH):
                        part = (j % 4) * 2 * HD
                        for g in range(IMGS):
                            ins = pe.matmul(bank[4][part:part + 2 * HD, (j // 4) * TOK + g * SEQ:(j // 4) * TOK + (g + 1) * SEQ],
                                            v_bd[:, g, j * 2 * HD:(j + 1) * 2 * HD],
                                            pT[:, j, g * SEQ:(g + 1) * SEQ], start=True, stop=True)
                    ins.then_inc(done["mm_ctx"], 1)
                if a:
                    pe.wait_ge(done["q"], KC * (i + 1))
                    mm3(bank[0][0:TOK, 0:DIM], hT, [(wa_hi[:, WV, j, :], wa_lo[:, WV, j, :]) for j in range(KC)])\
                        .then_inc(done["mm_v"], 1)
                if c:
                    pe.wait_ge(done["hot"], i - 1)
                    pe.wait_ge(done["acc"], EXPERTS * (i - 2) + 4)
                    pe.transpose(bank[3][0:EXPERTS, 0:TOK], hot[:], idtok).then_inc(done["mm_hotT"], 1)
                if a:
                    pe.wait_ge(done["k"], i + 1)
                    pe.wait_ge(done["q_lo"], KC * IMGS * (i + 1))
                    qd = [tuple(diag(t, j) for t in (q_hi, q_lo)) for j in range(KC)]
                    for m in range(KC):
                        o = bank[1][:, m * TOK:(m + 1) * TOK].rearrange("p (g t) -> p g t", g=IMGS)
                        mm3(o, [(wa_hi[:, WFQ, j, m * 128:(m + 1) * 128],
                                 wa_lo[:, WFQ, j, m * 128:(m + 1) * 128]) for j in range(KC)], qd)
                    pe.wait_ge(done["glo"], i + 1)
                    for m in range(KC):
                        for j in range(KC):
                            ins = pe.matmul(bank[1][:, KC * TOK + m * IMGS:KC * TOK + (m + 1) * IMGS],
                                            wa[:, WFG, j, m * 128:(m + 1) * 128], glo[:, j * IMGS:(j + 1) * IMGS],
                                            start=(j == 0), stop=(j == KC - 1))
                    ins.then_inc(done["mm_c"], 1)
                if c:
                    pe.wait_ge(done["hotT"], i - 1)
                    experts(3)
                if b:
                    pe.wait_ge(done["ctx_lo"], i)
                    mm3(bank[5][0:TOK, 0:DIM], [(ctx_hi[:, j, :], ctx_lo[:, j, :]) for j in range(KC)],
                        [(wa_hi[:, WO, j, :], wa_lo[:, WO, j, :]) for j in range(KC)]).then_inc(done["mm_o"], 1)
                if c:
                    pe.wait_ge(done["acc"], EXPERTS * (i - 2) + 6)
                    pe.matmul(bank[2][0:TOK, 0:DIM], hotT[:], fold_bias[:], start=True, stop=True)\
                        .then_inc(done["mm_fbias"], 1)
                if a:
                    pe.wait_ge(done["cth"], i + 1)
                    pe.wait_ge(done["v_s"], i + 1)
                    for j in range(KC):
                        ins = pe.matmul(bank[0][0:TOK, 0:2 * HEADS], cth[:, j, :], upz[:, j, :],
                                        start=(j == 0), stop=(j == KC - 1))
                    ins.then_inc(done["mm_pz"], 1)
                    wait_apart(pe, done["sp_lo"], i + 1, done["jmat"])
                    pe.transpose(bank[1][0:4 * HEADS, 0:TOK], sp4[:], idtok).then_inc(done["mm_spT"], 1)

            def diag(t, j):
                base = t[:, j, 0, 0:SEQ]
                return bass.AP(base.tensor, base.offset, [base.ap[0], [TOK + SEQ, IMGS], [1, SEQ]])

            run(pe, iteration)

        @block.vector
        def _(dve):
            def stats(in_ap, st, s_st, mv, s_mv, ve, s_ve, n):
                dve.bn_stats(st, in_ap).then_inc(s_st, 1)
                wait_apart(dve, s_st, n, done["ve1"])
                dve.bn_aggr(mv[:], st).then_inc(s_mv, 1)
                dve.wait_ge(s_mv, n)
                dve.tensor_scalar(ve[:], mv[:, 1:2], EPS, None, ALU.add).then_inc(s_ve, 1)

            def normalise(o, in_ap, mv, rs, s_rs, n, result):
                dve.wait_ge(s_rs, n)
                dve.tensor_scalar(o, in_ap, mv[:, 0:1], rs[:], ALU.subtract, ALU.mult).then_inc(result, 1)

            def ln1(n):
                dve.wait_ge(done["ld_x"], 16 * n)
                for c in range(2):
                    ins = dve.bn_stats(st1[:, c, :], xt[:, c * 384:(c + 1) * 384])
                ins.then_inc(done["st1"], 1)
                wait_apart(dve, done["st1"], n, done["ve1"])
                dve.bn_aggr(mv1[:], st1[:].rearrange("p a b -> p (a b)")).then_inc(done["mv1"], 1)
                dve.wait_ge(done["mv1"], n)
                dve.tensor_scalar(ve1[:], mv1[:, 1:2], EPS, None, ALU.add).then_inc(done["ve1"], 1)

            ln1(1)
            dve.wait_ge(done["ld_col"], 16)
            dve.tensor_scalar(bk4[:], col[:, L_BK:L_BK + KC], 0.25, None, ALU.mult).then_inc(done["bias_cols"], 1)
            dve.tensor_tensor(bf[:], col[:, L_BFQ:L_BFQ + KC], col[:, L_BFG:L_BFG + KC], ALU.add)\
                .then_inc(done["bias_cols"], 1)
            normalise(xn[:], xt[:], mv1, rs1, done["rs1"], 1, done["xn"])
            dve.wait_ge(done["ld_wp"], 16)
            for j in range(PC):
                dve.wait_ge(done["wp_hi"], j + 1)
                dve.scalar_tensor_tensor(wp_lo[:, j, :], wp[:, j, :], col[:, L_G1 + j:L_G1 + j + 1],
                                         wp_hi[:, j, :].bitcast(F32), ALU.mult, ALU.subtract).then_inc(done["wp_lo"], 1)
            dve.wait_ge(done["ld_row"], 16)
            dve.wait_ge(done["mm_bias1"], 1)
            dve.tensor_tensor(bias1[:], bank[4][0:TOK, 0:DIM], row[:, R_BIAS:R_BIAS + DIM], ALU.add)\
                .then_inc(done["bias1"], 1)
            dve.wait_ge(done["mm_extra"], 1)
            dve.tensor_tensor(extra[:], bank[6][0:TOK, 0:DIM], pe_pos, ALU.add).then_inc(done["extra"], 1)

            def rest_of_weights():
                dve.wait_ge(done["ld_wa"], 16)
                for j in range(5):
                    dve.wait_ge(done["wa_hi"], j + 1)
                    dve.tensor_tensor(wa_lo[:, j], wa[:, j], wa_hi[:, j].bitcast(F32), ALU.subtract)\
                        .then_inc(done["wa_lo"], 1)
                dve.wait_ge(done["gate_hi"], 1)
                dve.tensor_tensor(gate_lo[:], gate, gate_hi[:].bitcast(F32), ALU.subtract).then_inc(done["gate_lo"], 1)
                dve.wait_ge(done["mm_bias_o"], 1)
                dve.tensor_tensor(bias_o[:], bank[5][0:TOK, 0:DIM], row[:, R_BO:R_BO + DIM], ALU.add)\
                    .then_inc(done["bias_o"], 1)
                dve.wait_ge(done["mm_fb"], 1)
                dve.tensor_tensor(fold_bias[:], bank[7][0:EXPERTS, 0:DIM], row[0:EXPERTS, R_OB:R_OB + DIM], ALU.add)\
                    .then_inc(done["fold_bias"], 1)

            def fold_lo_part(e0, e1):
                for e in range(e0, e1):
                    dve.wait_ge(done["fold_hi"], e + 1)
                    o, hi = (t[:, e].rearrange("p k d -> p (k d)") for t in (fold_lo, fold_hi))
                    dve.tensor_tensor(o, bank[2 + e % 2][:, :], hi.bitcast(F32), ALU.subtract).then_inc(done["fold_lo"], 1)

            def split_lo(t_lo, t_hi, psum, s_hi, n, result):
                dve.wait_ge(s_hi, n)
                dve.tensor_tensor(t_lo, psum, t_hi.bitcast(F32), ALU.subtract).then_inc(result, 1)

            def flat(t):
                return t.rearrange("p c t -> p (c t)")

            def iteration(i, a, b, c):
                def experts(n):
                    dve.wait_ge(done["mm_f"], 4 * (i - 2) + n + 1)
                    for e in (2 * n, 2 * n + 1):
                        if e:
                            dve.wait_ge(done["acc"], EXPERTS * (i - 2) + e)
                        before = h2[:] if e == 0 else acc[:, (e - 1) % 2, :]
                        dve.scalar_tensor_tensor(acc[:, e % 2, :], bank[2 + n % 2][0:TOK, (e % 2) * DIM:(e % 2 + 1) * DIM],
                                                 hot[:, e:e + 1], before, ALU.mult, ALU.add).then_inc(done["acc"], 1)

                if a:
                    for n in range(2):
                        split_lo(flat(xT_lo[:, 3 * n:3 * n + 3, :]), flat(xT_hi[:, 3 * n:3 * n + 3, :]),
                                 bank[n][:, 0:3 * TOK], done["xT_hi"], 2 * i + n + 1, done["xT_lo"])
                if c:
                    dve.wait_ge(done["h2"], i - 1)
                    stats(h2[:], st4[:], done["st4"], mv4, done["mv4"], ve4, done["ve4"], i - 1)
                    normalise(un[:], h2[:], mv4, rs4, done["rs4"], i - 1, done["un"])
                if b:
                    for n in range(2):
                        dve.wait_ge(done["mm_s"], 2 * (i - 1) + n + 1)
                        dve.wait_ge(done["sq"], 2 * (i - 1) + n + 1)
                        dve.tensor_tensor(sc[:, n * HH:(n + 1) * HH, :].rearrange("p a b -> p (a b)"),
                                          bank[4 + n][0:TOK, 0:HALF],
                                          sq[:, n * HH:(n + 1) * HH, :].rearrange("p a b -> p (a b)"),
                                          ALU.subtract).then_inc(done["sc"], 1)
                    dve.wait_ge(done["sc"], 2 * i)
                    dve.tensor_reduce(smax[:], sc[:], AX.X, ALU.max).then_inc(done["smax"], 1)
                if a:
                    if isinstance(i, int) and i == 0:
                        dve.wait_ge(done["bias1"], 1)
                        dve.wait_ge(done["extra"], 1)
                    dve.wait_ge(done["mm_y"], i + 1)
                    dve.tensor_tensor(y[:], bank[0][0:TOK, 0:DIM], bias1[:], ALU.add).then_inc(done["y"], 1)
                    dve.wait_ge(done["y"], i + 1)
                    stats(y[:], st2[:], done["st2"], mv2, done["mv2"], ve2, done["ve2"], i + 1)
                if c:
                    split_lo(flat(uT_lo[:]), flat(uT_hi[:]), bank[2][:, 0:KC * TOK], done["uT_hi"], i - 1, done["uT_lo"])
                if a:
                    dve.scalar_tensor_tensor(yg[:], y[:], mv2[:, 0:1], row[:, R_G2:R_G2 + DIM],
                                             ALU.subtract, ALU.mult).then_inc(done["yg"], 1)
                    dve.wait_ge(done["rs2"], i + 1)
                    dve.tensor_tensor(rs2m[:], rs2[:], patch_mask, ALU.mult).then_inc(done["rs2m"], 1)
                    dve.wait_ge(done["rs2m"], i + 1)
                    free(dve, done["h_res"], i)
                    dve.scalar_tensor_tensor(h[:], yg[:], rs2m[:], extra[:], ALU.mult, ALU.add).then_inc(done["h"], 1)
                    dve.wait_ge(done["h"], i + 1)
                    stats(h[:], st3[:], done["st3"], mv3, done["mv3"], ve3, done["ve3"], i + 1)
                if b:
                    dve.wait_ge(done["ex"], i)
                    dve.tensor_reduce(ssum[:], ex[:], AX.X, ALU.add).then_inc(done["ssum"], 1)
                    dve.wait_ge(done["ssum"], i)
                    dve.reciprocal(rsum[:], ssum[:]).then_inc(done["rsum"], 1)
                if a:
                    normalise(hn[:], h[:], mv3, rs3, done["rs3"], i + 1, done["hn"])
                if isinstance(i, int) and i == 0:
                    rest_of_weights()
                if isinstance(i, int) and i < 2:
                    fold_lo_part(4 * i, 4 * i + 4)
                if c:
                    dve.wait_ge(done["mm_lg"], i - 1)
                    dve.tensor_tensor(logit[:], bank[3][0:TOK, 0:EXPERTS], row[:, R_GB:R_GB + EXPERTS], ALU.add)\
                        .then_inc(done["logit"], 1)
                    wait_apart(dve, done["logit"], i - 1, done["ve1"])
                    dve.max(top[:], logit[:]).then_inc(done["top"], 1)
                    wait_apart(dve, done["top"], i - 1, done["ve1"])
                    dve.max_index(topi[:], top[:], logit[:]).then_inc(done["topi"], 1)
                    dve.wait_ge(done["topi"], i - 1)
                    dve.tensor_copy(topf[:], topi[:, 0:1]).then_inc(done["topf"], 1)
                    dve.wait_ge(done["topf"], i - 1)
                    dve.tensor_scalar(hot[:], iota8, topf[:], None, ALU.is_equal).then_inc(done["hot"], 1)
                    dve.wait_ge(done["hot"], i - 1)
                    experts(0)
                    experts(1)
                if a:
                    split_lo(flat(hT_lo[:]), flat(hT_hi[:]), bank[1][:, 0:KC * TOK], done["hT_hi"], i + 1, done["hT_lo"])
                if b:
                    dve.wait_ge(done["mm_pT"], 2 * i)
                    dve.wait_ge(done["pT"], 2 * (i - 1) + 1)
                    dve.tensor_copy(pT[:, HH // 2:HH, :].rearrange("p c t -> p (c t)"),
                                    bank[7][0:PAIR, 0:HH // 2 * TOK]).then_inc(done["pT"], 1)
                if c:
                    experts(2)
                if a:
                    dve.wait_ge(done["mm_k"], i + 1)
                    if isinstance(i, int) and i == 0:
                        dve.wait_ge(done["bias_cols"], 2)
                    for m in range(KC):
                        ins = dve.tensor_scalar(k[:, m, :], bank[1][:, m * TOK:(m + 1) * TOK], 0.25, bk4[:, m:m + 1],
                                                ALU.mult, ALU.add)
                    ins.then_inc(done["k"], 1)
                    dve.wait_ge(done["k"], i + 1)
                    free(dve, done["k_bd"], 16 * HH * i)
                    dve.tensor_copy(k_s[:, 0], k[:]).then_inc(done["k_hi"], 1)
                    dve.wait_ge(done["k_hi"], i + 1)
                    dve.tensor_tensor(k_s[:, 1], k[:], k_s[:, 0].bitcast(F32), ALU.subtract).then_inc(done["k_lo"], 1)
                    dve.wait_ge(done["q"], KC * (i + 1))
                    dve.tensor_reduce(gsum[:], q[:].rearrange("p k (g t) -> p (k g) t", g=IMGS), AX.X, ALU.add)\
                        .then_inc(done["gsum"], 1)
                    dve.wait_ge(done["gsum"], i + 1)
                    dve.tensor_scalar(glo[:], gsum[:], 1.0 / SEQ, None, ALU.mult).then_inc(done["glo"], 1)
                if c:
                    dve.wait_ge(done["mm_hotT"], i - 1)
                    dve.tensor_copy(hotT[:], bank[3][0:EXPERTS, 0:TOK]).then_inc(done["hotT"], 1)
                if b:
                    split_lo(flat(ctx_lo[:]), flat(ctx_hi[:]), bank[4][:, 0:KC * TOK], done["ctx_hi"], i, done["ctx_lo"])
                if a:
                    dve.wait_ge(done["mm_c"], i + 1)
                    dve.tensor_tensor(gbias[:], bank[1][:, KC * TOK:KC * (TOK + IMGS)].rearrange("p (k g) -> p k g", k=KC),
                                      bf[:].unsqueeze(2).to_broadcast([128, KC, IMGS]), ALU.add).then_inc(done["gbias"], 1)
                    dve.wait_ge(done["gbias"], i + 1)
                    dve.tensor_tensor(cpre[:].rearrange("p k (g t) -> p (k g) t", g=IMGS),
                                      bank[1][:, 0:KC * TOK].rearrange("p (a t) -> p a t", t=SEQ),
                                      gbias[:].rearrange("p k g -> p (k g)").unsqueeze(2).to_broadcast([128, KC * IMGS, SEQ]),
                                      ALU.add).then_inc(done["cpre"], 1)
                if c:
                    experts(3)
                if b:
                    dve.wait_ge(done["mm_o"], i)
                    dve.wait_ge(done["h_res"], i)
                    dve.tensor_tensor(h2[:], bank[5][0:TOK, 0:DIM],
                                      h_res[:, bass.ds(i - 1, 1), :].rearrange("p a d -> p (a d)"), ALU.add)\
                        .then_inc(done["h2"], 1)
                if c:
                    dve.wait_ge(done["mm_fbias"], i - 1)
                    dve.wait_ge(done["acc"], EXPERTS * (i - 1))
                    free(dve, done["stored"], 16 * (i - 2))
                    dve.tensor_tensor(res[:], bank[2][0:TOK, 0:DIM], acc[:, (EXPERTS - 1) % 2, :], ALU.add)\
                        .then_inc(done["res"], 1)
                if a:
                    dve.wait_ge(done["epz"], i + 1)
                    dve.tensor_scalar(epz1[:], epz[:], 1.0, None, ALU.add).then_inc(done["epz1"], 1)
                    dve.wait_ge(done["epz1"], i + 1)
                    dve.reciprocal(rp[:], epz1[:, HEADS:2 * HEADS]).then_inc(done["rp"], 1)
                    dve.tensor_scalar(sp[:, 0:HEADS], epz1[:, 0:HEADS], ROOT2 / SEQ, None, ALU.mult).then_inc(done["sps"], 1)
                    dve.wait_ge(done["rp"], i + 1)
                    dve.scalar_tensor_tensor(sp[:, HEADS:2 * HEADS], epz1[:, 0:HEADS], -ROOT2, rp[:],
                                             ALU.mult, ALU.mult).then_inc(done["spn"], 1)
                    dve.wait_ge(done["spn"], i + 1)
                    dve.tensor_copy(sp4r[:], sp[:]).then_inc(done["sp_hi"], 1)
                    dve.wait_ge(done["sp_hi"], i + 1)
                    free(dve, done["mm_spT"], i)
                    dve.tensor_copy(sp4[:, 0:2 * HEADS], sp4r[:].bitcast(F32)).then_inc(done["sp_hic"], 1)
                    dve.tensor_tensor(sp4[:, 2 * HEADS:4 * HEADS], sp[:], sp4r[:].bitcast(F32), ALU.subtract)\
                        .then_inc(done["sp_lo"], 1)
                    dve.wait_ge(done["mm_spT"], i + 1)
                    dve.tensor_copy(spT[:], bank[1][0:4 * HEADS, 0:TOK]).then_inc(done["spT"], 1)
                    if not (isinstance(i, int) and i == TILES - 1):
                        ln1(i + 2)
                        normalise(xn[:], xt[:], mv1, rs1, done["rs1"], i + 2, done["xn"])

            run(dve, iteration)


def _constants():
    c = np.zeros((128, C_END), np.float32)
    c[:, C_ID:C_ID + 128] = np.eye(128)
    omega = np.arange(DIM // 4, dtype=np.float32) / np.float32(DIM // 4 - 1)
    omega = (np.float32(1.0) / np.float32(10000.0) ** omega).astype(np.float32)
    yy, xx = np.meshgrid(np.arange(GRID), np.arange(GRID), indexing="ij")
    yo = yy.reshape(-1)[:, None].astype(np.float32) * omega[None]
    xo = xx.reshape(-1)[:, None].astype(np.float32) * omega[None]
    pe = np.concatenate((np.sin(xo), np.cos(xo), np.sin(yo), np.cos(yo)), axis=1)
    for g in range(IMGS):
        c[g * SEQ + 2:(g + 1) * SEQ, C_PE:C_PE + DIM] = pe
        c[g * SEQ + 2:(g + 1) * SEQ, C_MASK] = 1.0
        c[0, C_SEL + g * SEQ + 2:C_SEL + (g + 1) * SEQ] = 1.0
        c[1, C_SEL + g * SEQ] = 1.0
        c[2:4, C_SEL + g * SEQ + 1] = 1.0
    for hd in range(HEADS):
        at = slice(C_J + hd * SEQ, C_J + (hd + 1) * SEQ)
        for part in range(2):
            c[2 * HEADS * part + hd, at] = np.arange(SEQ)
            c[2 * HEADS * part + HEADS + hd, at] = 1.0
    c[:, C_IOTA:C_IOTA + EXPERTS] = np.arange(EXPERTS)
    return c


def kernel(**inputs):
    import concourse.bacc as bacc
    from concourse.bass_utils import run_bass_kernel_spmd

    t = {k: np.asarray(v) for k, v in inputs.items()}
    f = np.float32

    x = t["x"].reshape(BATCH, CH, GRID, PATCH, GRID, PATCH).transpose(0, 2, 4, 1, 3, 5).reshape(BATCH, GRID * GRID, PDIM)
    xr = np.zeros((TILES * IMGS, SEQ, PDIM), f)
    xr[:BATCH, 2:] = x

    def chunks(w):
        return w.reshape(-1, 128, *w.shape[1:]).swapaxes(0, 1)

    def patch_order(w):
        return w.reshape(PATCH * PATCH, CH, *w.shape[1:]).swapaxes(0, 1).reshape(PDIM, *w.shape[1:])

    cols = np.zeros((128, L_END), f)
    cols[:, L_G1:L_G1 + PC] = chunks(patch_order(t["L0_tok_ln1_g"]))
    cols[:, L_B1:L_B1 + PC] = chunks(patch_order(t["L0_tok_ln1_b"]))
    for at, name in ((L_BQ, "bq"), (L_BK, "bk"), (L_BFQ, "bfq"), (L_BFG, "bfg"), (L_BV, "bv")):
        cols[:, at:at + KC] = chunks(t["L0_attn_" + name])
    upz = np.zeros((DIM, 2 * HEADS), f)
    for hd in range(HEADS):
        upz[hd * HD:(hd + 1) * HD, hd] = t["L0_attn_uz"][hd, 0]
        upz[hd * HD:(hd + 1) * HD, HEADS + hd] = t["L0_attn_up"][hd, 0]
    cols[:, L_UPZ:L_UPZ + KC * 2 * HEADS] = chunks(upz).reshape(128, -1)
    cols[:, L_GATE:L_GATE + KC * EXPERTS] = chunks(t["L0_ffn_gate_w"]).reshape(128, -1)
    cols[:, L_EB:L_EB + HC * EXPERTS] = chunks(np.ascontiguousarray(t["L0_ffn_expert_b"].T)).reshape(128, -1)
    rows = np.concatenate([t["L0_tok_bias"], t["L0_tok_ln2_g"], t["L0_attn_bo"], t["L0_ffn_out_b"],
                           t["L0_ffn_gate_b"]])[None]
    heads4 = np.concatenate([t["L0_tok_ln2_b"][None], t["cls_tok"][0], t["L0_tok_cls_token"][0],
                             t["L0_tok_cls_pos_embedding"][0]])
    w_attn = np.stack([chunks(t["L0_attn_" + n]) for n in ("wq", "wk", "wv", "wfq", "wo", "wfg")], axis=1)
    w_exp = t["L0_ffn_expert_w"].transpose(2, 0, 1).reshape(HC, 128, EXPERTS, DIM).transpose(1, 0, 2, 3)

    arrays = {
        "x_in": xr.reshape(TILES * TOK, PDIM), "w_patch": chunks(patch_order(t["L0_tok_W"])), "w_attn": w_attn,
        "w_exp": w_exp, "w_out": chunks(t["L0_ffn_out_w"]), "consts": _constants(), "cols": cols, "rows": rows,
        "heads4": heads4,
    }
    nc = bacc.Bacc("TRN2", target_bir_lowering=False, num_devices=1)
    arrays = {k: np.ascontiguousarray(v) for k, v in arrays.items()}
    args = [nc.dram_tensor(k, v.shape, F32, kind="ExternalInput").ap() for k, v in arrays.items()]
    args.append(nc.dram_tensor("out", (TILES * TOK, DIM), F32, kind="ExternalOutput").ap())
    vit_tower(nc, *args)
    r = run_bass_kernel_spmd(nc, [arrays], core_ids=[0])
    return r.results[0]["out"][:BATCH * SEQ].reshape(BATCH, SEQ, DIM)
```

```python
import numpy as np
import concourse.bass as bass
from concourse import mybir
from concourse.alu_op_type import AluOpType as ALU
from contextlib import ExitStack

F32 = mybir.dt.float32
F32R = mybir.dt.float32r
U32 = mybir.dt.uint32
ACT = mybir.ActivationFunctionType
AX = mybir.AxisListType

BATCH, CH, IMG, PATCH = 32, 3, 96, 16
GRID = IMG // PATCH
DIM = 256
PDIM = CH * PATCH * PATCH
KC = DIM // 128
PC = PDIM // 128
SEQ = GRID * GRID + 2
HEADS, HD = 16, 16
HH = HEADS // 2
EXPERTS, HID = 8, 512
HC = HID // 128
IMGS = 3
TOK = IMGS * SEQ
TILES = -(-BATCH // IMGS)
EPS = 1e-5
PAIR = 2 * SEQ
HALF = HH * SEQ
ROOT2 = float(np.sqrt(2.0))

C_ID, C_PE, C_J, C_MASK, C_IOTA, C_SEL = 0, 128, 384, 992, 993, 1001
C_END = C_SEL + TOK
L_G1, L_B1, L_BQ, L_BK, L_BFQ, L_BFG, L_BV = 0, 6, 12, 14, 16, 18, 20
L_UPZ, L_GATE, L_EB = 22, 86, 102
L_END = L_EB + HC * EXPERTS
R_BIAS, R_G2, R_BO, R_OB, R_GB = 0, 256, 512, 768, 1024
R_END = 1032


def vit_tower(nc, x, w_patch, w_attn, w_exp, w_out, consts, cols, rows, heads4, out):
    es = ExitStack()
    with es:
        def sb(name, shape, dt=F32):
            return es.enter_context(nc.sbuf_tensor(name, shape, dt))

        def sem(name):
            return es.enter_context(nc.semaphore(name))

        cst = sb("cst", [128, C_END])
        col = sb("col", [128, L_END])
        row = sb("row", [TOK, R_END])
        head4 = sb("head4", [4, DIM])
        wp = sb("wp", [128, PC, DIM])
        wp_hi = sb("wp_hi", [128, PC, DIM], F32R)
        wp_lo = sb("wp_lo", [128, PC, DIM], F32R)
        wa = sb("wa", [128, 6, KC, DIM])
        wa_hi = sb("wa_hi", [128, 6, KC, DIM], F32R)
        wa_lo = sb("wa_lo", [128, 6, KC, DIM], F32R)
        WQ, WK, WV, WFQ, WO, WFG = range(6)
        gate_hi = sb("gate_hi", [128, KC, EXPERTS], F32R)
        gate_lo = sb("gate_lo", [128, KC, EXPERTS], F32R)
        wexp = sb("wexp", [128, HC, 4, DIM])
        wout = sb("wout", [128, HC, DIM])
        fold_hi = sb("fold_hi", [128, EXPERTS, KC, DIM], F32R)
        fold_lo = sb("fold_lo", [128, EXPERTS, KC, DIM], F32R)
        fold_bias = sb("fold_bias", [EXPERTS, DIM])
        jmat = sb("jmat", [4 * HEADS, HEADS * SEQ], F32R)
        bias1 = sb("bias1", [TOK, DIM])
        extra = sb("extra", [TOK, DIM])
        bias_o = sb("bias_o", [TOK, DIM])
        nhalf = sb("nhalf", [TOK, 1])
        bk4 = sb("bk4", [128, KC])
        bf = sb("bf", [128, KC])
        xt = sb("xt", [TOK, PDIM])
        xn = sb("xn", [TOK, PDIM])
        st1 = sb("st1", [TOK, 2, 6])
        mv1 = sb("mv1", [TOK, 2])
        ve1 = sb("ve1", [TOK, 1])
        rs1 = sb("rs1", [TOK, 1])
        xT_hi = sb("xT_hi", [128, PC, TOK], F32R)
        xT_lo = sb("xT_lo", [128, PC, TOK], F32R)
        y = sb("y", [TOK, DIM])
        st2 = sb("st2", [TOK, 6])
        mv2 = sb("mv2", [TOK, 2])
        ve2 = sb("ve2", [TOK, 1])
        rs2 = sb("rs2", [TOK, 1])
        gamma2 = sb("gamma2", [TOK, DIM])
        yg = sb("yg", [TOK, DIM])
        h = sb("h", [TOK, DIM])
        h_res = sb("h_res", [TOK, DIM])
        st3 = sb("st3", [TOK, 6])
        mv3 = sb("mv3", [TOK, 2])
        ve3 = sb("ve3", [TOK, 1])
        rs3 = sb("rs3", [TOK, 1])
        hn = sb("hn", [TOK, DIM])
        hT_hi = sb("hT_hi", [128, KC, TOK], F32R)
        hT_lo = sb("hT_lo", [128, KC, TOK], F32R)
        q = sb("q", [128, KC, TOK])
        q_hi = sb("q_hi", [128, KC, IMGS, TOK], F32R)
        q_lo = sb("q_lo", [128, KC, IMGS, TOK], F32R)
        k = sb("k", [128, KC, TOK])
        k_s = sb("k_s", [128, 2, KC, TOK], F32R)
        k_bd = sb("k_bd", [128, 2 * KC, HH, TOK], F32R)
        v_s = sb("v_s", [TOK, 2, HH, 2, HD])
        v_bd = sb("v_bd", [PAIR, IMGS, DIM])
        gsum = sb("gsum", [128, KC, IMGS])
        glo_hi = sb("glo_hi", [128, KC, IMGS], F32R)
        glo_lo = sb("glo_lo", [128, KC, IMGS], F32R)
        cth = sb("cth", [128, KC, TOK])
        epz = sb("epz", [TOK, 2 * HEADS])
        epz1 = sb("epz1", [TOK, HEADS])
        rp = sb("rp", [TOK, HEADS])
        sp = sb("sp", [TOK, 2 * HEADS])
        sp4 = sb("sp4", [TOK, 4 * HEADS], F32R)
        spT = sb("spT", [4 * HEADS, TOK], F32R)
        sq = sb("sq", [TOK, HEADS, SEQ])
        sc = sb("sc", [TOK, HEADS, SEQ])
        smax = sb("smax", [TOK, HEADS])
        sd = sb("sd", [TOK, HEADS, SEQ])
        ex = sb("ex", [TOK, HEADS, SEQ])
        ssum = sb("ssum", [TOK, HEADS])
        rsum = sb("rsum", [TOK, HEADS])
        pr = sb("pr", [TOK, HEADS, SEQ])
        pT = sb("pT", [PAIR, HH, TOK])
        ctx_hi = sb("ctx_hi", [128, KC, TOK], F32R)
        ctx_lo = sb("ctx_lo", [128, KC, TOK], F32R)
        h2 = sb("h2", [TOK, DIM])
        st4 = sb("st4", [TOK, 6])
        mv4 = sb("mv4", [TOK, 2])
        ve4 = sb("ve4", [TOK, 1])
        rs4 = sb("rs4", [TOK, 1])
        un = sb("un", [TOK, DIM])
        uT_hi = sb("uT_hi", [128, KC, TOK], F32R)
        uT_lo = sb("uT_lo", [128, KC, TOK], F32R)
        logit = sb("logit", [TOK, EXPERTS])
        top = sb("top", [TOK, 8])
        topi = sb("topi", [TOK, 8], U32)
        topf = sb("topf", [TOK, 1])
        hot = sb("hot", [TOK, EXPERTS])
        hotT = sb("hotT", [EXPERTS, TOK])
        acc = sb("acc", [TOK, 2, DIM])
        biases = sb("biases", [TOK, DIM])
        res = sb("res", [TOK, DIM])

        bank = [es.enter_context(nc.psum_tensor(f"bank{i}", [128, 512], F32)) for i in range(8)]

        ident = cst[:, C_ID:C_ID + 128]
        idtok = cst[0:TOK, C_ID:C_ID + TOK]
        pe_pos = cst[0:TOK, C_PE:C_PE + DIM]
        patch_mask = cst[0:TOK, C_MASK:C_MASK + 1]
        iota8 = cst[0:TOK, C_IOTA:C_IOTA + EXPERTS]
        sel4 = cst[0:4, C_SEL:C_SEL + TOK]
        upz = col[:, L_UPZ:L_UPZ + KC * 2 * HEADS].rearrange("p (k n) -> p k n", k=KC)
        gate = col[:, L_GATE:L_GATE + KC * EXPERTS].rearrange("p (k n) -> p k n", k=KC)
        ebT = col[:, L_EB:L_EB + HC * EXPERTS].rearrange("p (k n) -> p k n", k=HC)

        done = {name: sem("s_" + name) for name in """ld_cst ld_col ld_row ld_head4 ld_wp ld_wa ld_wout
            zeros nhalf bias_cols wp_hi wp_lo wa_hi wa_lo gate_hi gate_lo jmat
            mm_bias1 mm_bias_o mm_extra mm_fb bias1 bias_o extra gamma2 fold_bias
            mm_fold fold_hi fold_lo
            ld_x st1 mv1 ve1 rs1 xn mm_xT xT_hi xT_lo mm_y y st2 mv2 ve2 rs2 yg h h_res
            st3 mv3 ve3 rs3 hn mm_hT hT_hi hT_lo mm_q q q_hi q_lo mm_k k k_hi k_lo k_bd
            mm_v v_s v_bd gsum glo_hi glo_lo mm_c cth mm_pz epz epz1 rp sps spn sp_hi sp_lo mm_spT spT
            mm_g mm_s sq sc smax sd ex ssum rsum pr mm_pT pT mm_ctx ctx_hi ctx_lo mm_o h2
            st4 mv4 ve4 rs4 un mm_uT uT_hi uT_lo mm_lg logit top topi topf hot mm_f acc
            mm_hotT hotT mm_fbias biases res stored""".split()}

        ld_wexp = [sem(f"s_ld_wexp{n}") for n in range(2)]

        block = es.enter_context(nc.Block())

        def free(eng, semaphore, n):
            if not (isinstance(n, int) and n <= 0):
                eng.wait_ge(semaphore, n)

        def flat(t):
            return t.rearrange("p c t -> p (c t)")

        def diag(t, j):
            base = t[:, j, 0, 0:SEQ]
            return bass.AP(base.tensor, base.offset, [base.ap[0], [TOK + SEQ, IMGS], [1, SEQ]])

        def images(t, j):
            return t[:, j, :].rearrange("p (g t) -> p g t", g=IMGS)

        def wait_apart(eng, semaphore, n, settled):
            if not isinstance(n, int):
                eng.wait_ge(settled, 1)
            eng.wait_ge(semaphore, n)

        def has_next(i):
            return not (isinstance(i, int) and i >= TILES - 1)

        def run(eng, iteration):
            iteration(0, True, False, False)
            iteration(1, True, True, False)
            iteration(2, True, True, True)
            with eng.Fori(3, TILES - 2) as i:
                iteration(i, True, True, True)
            iteration(TILES - 2, True, True, True)
            iteration(TILES - 1, True, True, True)
            iteration(TILES, False, True, True)
            iteration(TILES + 1, False, False, True)

        @block.sync
        def _(sync):
            sync.dma_start(xt[:], x[0:TOK, :]).then_inc(done["ld_x"], 16)
            sync.dma_start(wp[:], w_patch).then_inc(done["ld_wp"], 16)
            sync.wait_ge(done["xn"], 1)
            sync.dma_start(xt[:], x[TOK:2 * TOK, :]).then_inc(done["ld_x"], 16)
            sync.dma_start(wa[:], w_attn).then_inc(done["ld_wa"], 16)

            def load_experts(n):
                if n >= 2:
                    sync.wait_ge(done["mm_fold"], 2 * n - 2)
                at = 2 * (n % 2)
                sync.dma_start(wexp[:, :, at:at + 2, :], w_exp[:, :, 2 * n:2 * n + 2, :]).then_inc(ld_wexp[n % 2], 16)

            load_experts(0)
            load_experts(1)

            def iteration(i, a, b, c):
                if a:
                    if isinstance(i, int) and i == 0:
                        load_experts(2)
                        load_experts(3)
                    if isinstance(i, int) and i == 0:
                        sync.wait_ge(done["zeros"], 4)
                    sync.wait_ge(done["k_lo"], i + 1)
                    free(sync, done["smax"], i)
                    for hd in range(HH):
                        part = slice(hd * HD, (hd + 1) * HD)
                        sync.dma_start(
                            k_bd[part, :, hd, :].bitcast(F32),
                            k_s[part].rearrange("p a k t -> p (a k) t").bitcast(F32)).then_inc(done["k_bd"], 16)
                    if not (isinstance(i, int) and i >= TILES - 2):
                        patches = x[bass.ds((i + 2) * TOK, TOK), :]
                        sync.wait_ge(done["xn"], i + 2)
                        sync.dma_start(xt[:], patches).then_inc(done["ld_x"], 16)
                    free(sync, done["mm_ctx"], i)
                    sync.wait_ge(done["v_s"], i + 1)
                    for g in range(IMGS):
                        for par in range(2):
                            sync.dma_start(v_bd[par * SEQ:(par + 1) * SEQ, g, :],
                                           v_s[g * SEQ:(g + 1) * SEQ, par].rearrange("p a b d -> p (a b d)"))\
                                .then_inc(done["v_bd"], 16)
                if c:
                    sync.wait_ge(done["res"], i - 1)
                    sync.dma_start(out[bass.ds((i - 2) * TOK, TOK), :], res[:]).then_inc(done["stored"], 16)

            run(sync, iteration)
            sync.wait_ge(done["stored"], 16 * TILES)

        @block.gpsimd
        def _(pool):
            pool.dma_start(cst[:], consts).then_inc(done["ld_cst"], 16)
            pool.memset(nhalf[:], -0.5).then_inc(done["nhalf"], 1)
            pool.memset(q_hi[:].bitcast(F32), 0.0).then_inc(done["zeros"], 1)
            pool.memset(q_lo[:].bitcast(F32), 0.0).then_inc(done["zeros"], 1)
            pool.memset(v_s[:], 0.0).then_inc(done["zeros"], 1)
            pool.memset(k_bd[:].bitcast(F32), 0.0).then_inc(done["zeros"], 1)
            pool.wait_ge(done["nhalf"], 1)

            def rstd(out_ap, in_ap, ready, result, n):
                pool.wait_ge(ready, n)
                pool.tensor_tensor(out_ap, in_ap, nhalf[:], ALU.pow).then_inc(result, 1)

            rstd(rs1[:], ve1[:], done["ve1"], done["rs1"], 1)

            def iteration(i, a, b, c):
                if a:
                    rstd(rs2[:], ve2[:], done["ve2"], done["rs2"], i + 1)
                    rstd(rs3[:], ve3[:], done["ve3"], done["rs3"], i + 1)
                if b:
                    pool.wait_ge(done["smax"], i)
                    pool.tensor_tensor(sd[:], sc[:], smax[:].unsqueeze(2).to_broadcast([TOK, HEADS, SEQ]),
                                       ALU.subtract).then_inc(done["sd"], 1)
                if b:
                    pool.wait_ge(done["rsum"], i)
                    free(pool, done["mm_pT"], 2 * (i - 1))
                    pool.tensor_tensor(pr[:], ex[:], rsum[:].unsqueeze(2).to_broadcast([TOK, HEADS, SEQ]),
                                       ALU.mult).then_inc(done["pr"], 1)
                if a:
                    pool.wait_ge(done["q_hi"], i + 1)
                    for j in range(KC):
                        pool.tensor_tensor(diag(q_lo, j), images(q, j), diag(q_hi, j).bitcast(F32),
                                           ALU.subtract).then_inc(done["q_lo"], 1)
                    if has_next(i):
                        rstd(rs1[:], ve1[:], done["ve1"], done["rs1"], i + 2)
                if b:
                    rstd(rs4[:], ve4[:], done["ve4"], done["rs4"], i)
                if a:
                    if isinstance(i, int) and i == 0:
                        pool.wait_ge(done["bias_o"], 1)
                    pool.wait_ge(done["h"], i + 1)
                    free(pool, done["h2"], i)
                    pool.tensor_tensor(h_res[:], h[:], bias_o[:], ALU.add).then_inc(done["h_res"], 1)

            run(pool, iteration)

        @block.scalar
        def _(act):
            act.dma_start(col[:], cols).then_inc(done["ld_col"], 16)
            act.dma_start(row[:], rows.to_broadcast([TOK, R_END])).then_inc(done["ld_row"], 16)
            act.dma_start(head4[:], heads4).then_inc(done["ld_head4"], 16)
            act.dma_start(wout[:], w_out).then_inc(done["ld_wout"], 16)

            act.wait_ge(done["ld_col"], 16)
            act.wait_ge(done["ld_wp"], 16)
            for j in range(PC):
                act.activation(wp_hi[:, j, :], wp[:, j, :], ACT.Copy,
                               scale=col[:, L_G1 + j:L_G1 + j + 1]).then_inc(done["wp_hi"], 1)
            act.wait_ge(done["ld_wa"], 16)
            for j in range(6):
                act.copy(wa_hi[:, j], wa[:, j]).then_inc(done["wa_hi"], 1)
            act.copy(gate_hi[:], gate).then_inc(done["gate_hi"], 1)
            act.wait_ge(done["ld_cst"], 16)
            act.copy(jmat[:], cst[0:4 * HEADS, C_J:C_J + HEADS * SEQ]).then_inc(done["jmat"], 1)

            def fold_hi_part(e0, e1):
                for e in range(e0, e1):
                    act.wait_ge(done["mm_fold"], e + 1)
                    act.copy(fold_hi[:, e].rearrange("p k d -> p (k d)"), bank[2 + e % 2][:, :]).then_inc(done["fold_hi"], 1)

            def patches_hi(n, tile):
                act.wait_ge(done["mm_xT"], 2 * tile + n + 1)
                if n == 0:
                    free(act, done["mm_y"], tile)
                act.copy(flat(xT_hi[:, 3 * n:3 * n + 3, :]), bank[n][:, 0:3 * TOK]).then_inc(done["xT_hi"], 1)

            def iteration(i, a, b, c):
                first = isinstance(i, int) and i == 0

                def exponentials():
                    act.wait_ge(done["sd"], i)
                    free(act, done["pr"], i - 1)
                    act.activation(ex[:], sd[:], ACT.Exp).then_inc(done["ex"], 1)

                if first:
                    patches_hi(0, 0)
                    patches_hi(1, 0)
                if b:
                    act.wait_ge(done["mm_spT"], i)
                    act.copy(spT[:], bank[7][0:4 * HEADS, 0:TOK]).then_inc(done["spT"], 1)
                if c:
                    act.wait_ge(done["mm_uT"], i - 1)
                    free(act, done["mm_f"], 4 * (i - 2))
                    act.copy(flat(uT_hi[:]), bank[2][:, 0:KC * TOK]).then_inc(done["uT_hi"], 1)
                if b:
                    for n in range(2):
                        act.wait_ge(done["mm_g"], 2 * (i - 1) + n + 1)
                        if n == 0:
                            free(act, done["sc"], 2 * (i - 1))
                        act.activation(flat(sq[:, n * HH:(n + 1) * HH, :]), bank[6 + n][0:TOK, 0:HALF], ACT.Square)\
                            .then_inc(done["sq"], 1)
                if isinstance(i, int) and i < 2:
                    if b:
                        exponentials()
                    fold_hi_part(4 * i, 4 * i + 4)
                if a:
                    act.wait_ge(done["mm_hT"], i + 1)
                    free(act, done["mm_v"], i)
                    act.copy(flat(hT_hi[:]), bank[0][:, 0:KC * TOK]).then_inc(done["hT_hi"], 1)
                if b and not (isinstance(i, int) and i < 2):
                    exponentials()
                if c:
                    act.wait_ge(done["mm_hotT"], i - 1)
                    free(act, done["mm_fbias"], i - 2)
                    act.copy(hotT[:], bank[7][0:EXPERTS, 0:TOK]).then_inc(done["hotT"], 1)
                if a:
                    act.wait_ge(done["mm_q"], i + 1)
                    if first:
                        act.wait_ge(done["bias_cols"], 2)
                        act.wait_ge(done["zeros"], 4)
                    for m in range(KC):
                        ins = act.activation(q[:, m, :], bank[0][:, m * TOK:(m + 1) * TOK], ACT.Identity,
                                             bias=col[:, L_BQ + m:L_BQ + m + 1])
                    ins.then_inc(done["q"], 1)
                    act.wait_ge(done["q"], i + 1)
                    for m in range(KC):
                        ins = act.copy(diag(q_hi, m), images(q, m))
                    ins.then_inc(done["q_hi"], 1)
                if c:
                    act.wait_ge(done["mm_fbias"], i - 1)
                    free(act, done["res"], i - 2)
                    act.copy(biases[:], bank[6][0:TOK, 0:DIM]).then_inc(done["biases"], 1)
                if a:
                    act.wait_ge(done["mm_k"], i + 1)
                    for m in range(KC):
                        ins = act.activation(k[:, m, :], bank[1][:, m * TOK:(m + 1) * TOK], ACT.Identity,
                                             bias=bk4[:, m:m + 1], scale=0.25)
                    ins.then_inc(done["k"], 1)
                    act.wait_ge(done["k"], i + 1)
                    free(act, done["k_bd"], 16 * HH * i)
                    act.copy(k_s[:, 0], k[:]).then_inc(done["k_hi"], 1)
                    act.wait_ge(done["mm_v"], i + 1)
                    free(act, done["v_bd"], 6 * 16 * i)
                    pv = bank[0][0:TOK, 0:DIM].rearrange("p (a b d) -> p a b d", a=HH, b=2)
                    for par in range(2):
                        ins = act.copy(v_s[:, par, :, par, :], pv[:, :, par, :])
                    ins.then_inc(done["v_s"], 1)
                if b:
                    for n in range(2):
                        act.wait_ge(done["mm_pT"], 2 * (i - 1) + n + 1)
                        if n == 0:
                            free(act, done["mm_ctx"], i - 1)
                        act.copy(flat(pT[:, n * HH // 2:(n + 1) * HH // 2, :]), bank[6 + n][0:PAIR, 0:HH // 2 * TOK])\
                            .then_inc(done["pT"], 1)
                if a:
                    act.wait_ge(done["mm_c"], i + 1)
                    for m in range(KC):
                        ins = act.activation(cth[:, m, :], bank[1][:, m * TOK:(m + 1) * TOK], ACT.Tanh, bias=bf[:, m:m + 1])
                    ins.then_inc(done["cth"], 1)
                if b:
                    act.wait_ge(done["mm_ctx"], i)
                    act.copy(flat(ctx_hi[:]), bank[4][:, 0:KC * TOK]).then_inc(done["ctx_hi"], 1)
                if a:
                    if has_next(i):
                        patches_hi(0, i + 1)
                    act.wait_ge(done["mm_pz"], i + 1)
                    act.activation(epz[:], bank[1][0:TOK, DIM:DIM + 2 * HEADS], ACT.Exp, scale=-1.0).then_inc(done["epz"], 1)
                    if has_next(i):
                        patches_hi(1, i + 1)

            run(act, iteration)

        @block.tensor
        def _(pe):
            def mm3(o, left, right):
                last = len(left) - 1
                for n, ((lh, ll), (rh, rl)) in enumerate(zip(left, right)):
                    pe.matmul(o, lh, rh, start=(n == 0), stop=False)
                    pe.matmul(o, lh, rl, start=False, stop=False)
                    ins = pe.matmul(o, ll, rh, start=False, stop=(n == last))
                return ins

            pe.wait_ge(done["ld_col"], 16)
            pe.wait_ge(done["ld_wp"], 16)
            for j in range(PC):
                ins = pe.matmul(bank[4][0:TOK, 0:DIM], col[:, L_B1 + j:L_B1 + j + 1].to_broadcast([128, TOK]),
                                wp[:, j, :], start=(j == 0), stop=(j == PC - 1))
            ins.then_inc(done["mm_bias1"], 1)
            pe.wait_ge(done["ld_cst"], 16)
            pe.wait_ge(done["ld_head4"], 16)
            pe.matmul(bank[6][0:TOK, 0:DIM], sel4, head4[:], start=True, stop=True).then_inc(done["mm_extra"], 1)
            pe.wait_ge(done["ld_wa"], 16)
            for j in range(KC):
                ins = pe.matmul(bank[5][0:TOK, 0:DIM], col[:, L_BV + j:L_BV + j + 1].to_broadcast([128, TOK]),
                                wa[:, WO, j, :], start=(j == 0), stop=(j == KC - 1))
            ins.then_inc(done["mm_bias_o"], 1)
            pe.wait_ge(done["ld_wout"], 16)
            for j in range(HC):
                ins = pe.matmul(bank[7][0:EXPERTS, 0:DIM], ebT[:, j, :], wout[:, j, :],
                                start=(j == 0), stop=(j == HC - 1))
            ins.then_inc(done["mm_fb"], 1)

            def fold(e0, e1):
                for e in range(e0, e1):
                    pe.wait_ge(ld_wexp[e // 2 % 2], 16 * (e // 4 + 1))
                    if e >= 2:
                        pe.wait_ge(done["fold_lo"], e - 1)
                    for m in range(KC):
                        for j in range(HC):
                            ins = pe.matmul(bank[2 + e % 2][:, m * DIM:(m + 1) * DIM],
                                            wexp[:, j, e % 4, m * 128:(m + 1) * 128], wout[:, j, :],
                                            start=(j == 0), stop=(j == HC - 1))
                    ins.then_inc(done["mm_fold"], 1)

            def transpose_patches(n, tile):
                pe.wait_ge(done["xn"], tile + 1)
                for j in range(3):
                    ins = pe.transpose(bank[n][:, j * TOK:(j + 1) * TOK],
                                       xn[:, (3 * n + j) * 128:(3 * n + j + 1) * 128], idtok)
                ins.then_inc(done["mm_xT"], 1)

            def iteration(i, a, b, c):
                first = isinstance(i, int) and i == 0
                hT = [(hT_hi[:, j, :], hT_lo[:, j, :]) for j in range(KC)]
                uT = [(uT_hi[:, j, :], uT_lo[:, j, :]) for j in range(KC)]

                def weights(which, m):
                    return [tuple(w[:, which, j, m * 128:(m + 1) * 128] for w in (wa_hi, wa_lo)) for j in range(KC)]

                def project(bk, which, result):
                    for m in range(KC):
                        ins = mm3(bank[bk][:, m * TOK:(m + 1) * TOK], weights(which, m), hT)
                    ins.then_inc(result, 1)

                def experts(n):
                    for e in (2 * n, 2 * n + 1):
                        ins = mm3(bank[2 + n % 2][0:TOK, (e % 2) * DIM:(e % 2 + 1) * DIM], uT,
                                  [(fold_hi[:, e, j, :], fold_lo[:, e, j, :]) for j in range(KC)])
                    ins.then_inc(done["mm_f"], 1)

                if first:
                    transpose_patches(0, 0)
                    transpose_patches(1, 0)
                    pe.wait_ge(done["wp_lo"], PC)
                if a:
                    pe.wait_ge(done["xT_lo"], 2 * (i + 1))
                    mm3(bank[0][0:TOK, 0:DIM], [(xT_hi[:, j, :], xT_lo[:, j, :]) for j in range(PC)],
                        [(wp_hi[:, j, :], wp_lo[:, j, :]) for j in range(PC)]).then_inc(done["mm_y"], 1)
                if b:
                    if isinstance(i, int) and i == 1:
                        pe.wait_ge(done["extra"], 1)
                        pe.wait_ge(done["fold_bias"], 1)
                    wait_apart(pe, done["sp_lo"], i, done["jmat"])
                    pe.transpose(bank[7][0:4 * HEADS, 0:TOK], sp4[:].bitcast(F32), idtok).then_inc(done["mm_spT"], 1)
                if c:
                    pe.wait_ge(done["un"], i - 1)
                    for j in range(KC):
                        ins = pe.transpose(bank[2][:, j * TOK:(j + 1) * TOK], un[:, j * 128:(j + 1) * 128], idtok)
                    ins.then_inc(done["mm_uT"], 1)
                if b:
                    pe.wait_ge(done["spT"], i)
                    for n in range(2):
                        pe.matmul(bank[6 + n][0:TOK, 0:HALF], spT[:], jmat[:, n * HALF:(n + 1) * HALF],
                                  start=True, stop=True).then_inc(done["mm_g"], 1)
                    pe.wait_ge(done["k_bd"], 16 * HH * i)
                    free(pe, done["h2"], i - 1)
                    for n in range(2):
                        o = bank[4 + n][0:TOK, 0:HALF].rearrange("p (a b) -> p a b", a=HH)
                        keys = [tuple(k_bd[:, KC * w + n, :, g * SEQ:(g + 1) * SEQ] for w in range(2))
                                for g in range(IMGS)]
                        mm3(o, [(q_hi[:, n, g, :], q_lo[:, n, g, :]) for g in range(IMGS)],
                            keys).then_inc(done["mm_s"], 1)
                if c:
                    pe.wait_ge(done["uT_lo"], i - 1)
                    free(pe, done["acc"], EXPERTS * (i - 2))
                    if isinstance(i, int) and i == 2:
                        pe.wait_ge(done["fold_lo"], EXPERTS)
                    mm3(bank[3][0:TOK, 0:EXPERTS], uT,
                        [(gate_hi[:, j, :], gate_lo[:, j, :]) for j in range(KC)]).then_inc(done["mm_lg"], 1)
                    experts(0)
                if isinstance(i, int) and i < 2:
                    fold(4 * i, 4 * i + 4)
                if a:
                    pe.wait_ge(done["hn"], i + 1)
                    for j in range(KC):
                        ins = pe.transpose(bank[0][:, j * TOK:(j + 1) * TOK], hn[:, j * 128:(j + 1) * 128], idtok)
                    ins.then_inc(done["mm_hT"], 1)
                if c:
                    pe.wait_ge(done["logit"], i - 1)
                    experts(1)
                    pe.wait_ge(done["hot"], i - 1)
                    pe.transpose(bank[7][0:EXPERTS, 0:TOK], hot[:], idtok).then_inc(done["mm_hotT"], 1)
                if a:
                    if first:
                        pe.wait_ge(done["wa_lo"], 6)
                    pe.wait_ge(done["hT_lo"], i + 1)
                    project(0, WQ, done["mm_q"])
                if c:
                    pe.wait_ge(done["hotT"], i - 1)
                    pe.matmul(bank[6][0:TOK, 0:DIM], hotT[:], fold_bias[:], start=True, stop=True)\
                        .then_inc(done["mm_fbias"], 1)
                if a:
                    project(1, WK, done["mm_k"])
                    pe.wait_ge(done["q"], i + 1)
                    mm3(bank[0][0:TOK, 0:DIM], hT, [(wa_hi[:, WV, j, :], wa_lo[:, WV, j, :]) for j in range(KC)])\
                        .then_inc(done["mm_v"], 1)
                if b:
                    if c:
                        pe.wait_ge(done["biases"], i - 1)
                    pe.wait_ge(done["pr"], i)
                    for n in range(2):
                        for j in range(HH // 2):
                            pair = flat(pr[:, (n * HH + 2 * j):(n * HH + 2 * j + 2), :])
                            ins = pe.transpose(bank[6 + n][0:PAIR, j * TOK:(j + 1) * TOK], pair, idtok)
                        ins.then_inc(done["mm_pT"], 1)
                if a:
                    pe.wait_ge(done["k"], i + 1)
                    pe.wait_ge(done["q_lo"], KC * (i + 1))
                    pe.wait_ge(done["glo_lo"], i + 1)
                    both = [tuple(diag(t, j) for t in (q_hi, q_lo)) for j in range(KC)] + \
                        [tuple(t[:, j, :].unsqueeze(2).to_broadcast([128, IMGS, SEQ]) for t in (glo_hi, glo_lo))
                         for j in range(KC)]
                    for m in range(KC):
                        o = bank[1][:, m * TOK:(m + 1) * TOK].rearrange("p (g t) -> p g t", g=IMGS)
                        ins = mm3(o, weights(WFQ, m) + weights(WFG, m), both)
                    ins.then_inc(done["mm_c"], 1)
                if b:
                    pe.wait_ge(done["pT"], 2 * i)
                    pe.wait_ge(done["v_bd"], 6 * 16 * i)
                    for j in range(HH):
                        part = (j % 4) * 2 * HD
                        for g in range(IMGS):
                            at = (j // 4) * TOK + g * SEQ
                            ins = pe.matmul(bank[4][part:part + 2 * HD, at:at + SEQ],
                                            v_bd[:, g, j * 2 * HD:(j + 1) * 2 * HD],
                                            pT[:, j, g * SEQ:(g + 1) * SEQ], start=True, stop=True)
                    ins.then_inc(done["mm_ctx"], 1)
                if a:
                    if has_next(i):
                        pe.wait_ge(done["v_s"], i + 1)
                        transpose_patches(0, i + 1)
                    pe.wait_ge(done["cth"], i + 1)
                    for j in range(KC):
                        ins = pe.matmul(bank[1][0:TOK, DIM:DIM + 2 * HEADS], cth[:, j, :], upz[:, j, :],
                                        start=(j == 0), stop=(j == KC - 1))
                    ins.then_inc(done["mm_pz"], 1)
                if c:
                    pe.wait_ge(done["acc"], EXPERTS * (i - 2) + 2)
                    experts(2)
                if b:
                    pe.wait_ge(done["ctx_lo"], i)
                    mm3(bank[5][0:TOK, 0:DIM], [(ctx_hi[:, j, :], ctx_lo[:, j, :]) for j in range(KC)],
                        [(wa_hi[:, WO, j, :], wa_lo[:, WO, j, :]) for j in range(KC)]).then_inc(done["mm_o"], 1)
                if a and has_next(i):
                    pe.wait_ge(done["epz"], i + 1)
                    transpose_patches(1, i + 1)
                if c:
                    pe.wait_ge(done["acc"], EXPERTS * (i - 2) + 4)
                    experts(3)

            run(pe, iteration)

        @block.vector
        def _(dve):
            def stats(in_ap, st, s_st, mv, s_mv, ve, s_ve, n):
                dve.bn_stats(st, in_ap).then_inc(s_st, 1)
                wait_apart(dve, s_st, n, done["ve1"])
                dve.bn_aggr(mv[:], st).then_inc(s_mv, 1)
                dve.wait_ge(s_mv, n)
                dve.tensor_scalar(ve[:], mv[:, 1:2], EPS, None, ALU.add).then_inc(s_ve, 1)

            def normalise(o, in_ap, mv, rs, s_rs, n, result):
                dve.wait_ge(s_rs, n)
                dve.tensor_scalar(o, in_ap, mv[:, 0:1], rs[:], ALU.subtract, ALU.mult).then_inc(result, 1)

            def ln1(n):
                dve.wait_ge(done["ld_x"], 16 * n)
                for c in range(2):
                    ins = dve.bn_stats(st1[:, c, :], xt[:, c * 384:(c + 1) * 384])
                ins.then_inc(done["st1"], 1)
                wait_apart(dve, done["st1"], n, done["ve1"])
                dve.bn_aggr(mv1[:], st1[:].rearrange("p a b -> p (a b)")).then_inc(done["mv1"], 1)
                dve.wait_ge(done["mv1"], n)
                dve.tensor_scalar(ve1[:], mv1[:, 1:2], EPS, None, ALU.add).then_inc(done["ve1"], 1)

            ln1(1)
            dve.wait_ge(done["ld_col"], 16)
            dve.tensor_scalar(bk4[:], col[:, L_BK:L_BK + KC], 0.25, None, ALU.mult).then_inc(done["bias_cols"], 1)
            dve.tensor_tensor(bf[:], col[:, L_BFQ:L_BFQ + KC], col[:, L_BFG:L_BFG + KC], ALU.add)\
                .then_inc(done["bias_cols"], 1)
            normalise(xn[:], xt[:], mv1, rs1, done["rs1"], 1, done["xn"])
            dve.wait_ge(done["ld_wp"], 16)
            for j in range(PC):
                dve.wait_ge(done["wp_hi"], j + 1)
                dve.scalar_tensor_tensor(wp_lo[:, j, :], wp[:, j, :], col[:, L_G1 + j:L_G1 + j + 1],
                                         wp_hi[:, j, :].bitcast(F32), ALU.mult, ALU.subtract).then_inc(done["wp_lo"], 1)
            dve.wait_ge(done["ld_row"], 16)
            dve.wait_ge(done["mm_bias1"], 1)
            dve.tensor_tensor(bias1[:], bank[4][0:TOK, 0:DIM], row[:, R_BIAS:R_BIAS + DIM], ALU.add)\
                .then_inc(done["bias1"], 1)
            dve.wait_ge(done["mm_extra"], 1)
            dve.tensor_tensor(extra[:], bank[6][0:TOK, 0:DIM], pe_pos, ALU.add).then_inc(done["extra"], 1)
            dve.tensor_scalar(gamma2[:], row[:, R_G2:R_G2 + DIM], patch_mask, None, ALU.mult).then_inc(done["gamma2"], 1)

            def rest_of_weights():
                dve.wait_ge(done["ld_wa"], 16)
                for j in range(6):
                    dve.wait_ge(done["wa_hi"], j + 1)
                    dve.tensor_tensor(wa_lo[:, j], wa[:, j], wa_hi[:, j].bitcast(F32), ALU.subtract)\
                        .then_inc(done["wa_lo"], 1)
                dve.wait_ge(done["gate_hi"], 1)
                dve.tensor_tensor(gate_lo[:], gate, gate_hi[:].bitcast(F32), ALU.subtract).then_inc(done["gate_lo"], 1)
                dve.wait_ge(done["mm_bias_o"], 1)
                dve.tensor_tensor(bias_o[:], bank[5][0:TOK, 0:DIM], row[:, R_BO:R_BO + DIM], ALU.add)\
                    .then_inc(done["bias_o"], 1)
                dve.wait_ge(done["mm_fb"], 1)
                dve.tensor_tensor(fold_bias[:], bank[7][0:EXPERTS, 0:DIM], row[0:EXPERTS, R_OB:R_OB + DIM], ALU.add)\
                    .then_inc(done["fold_bias"], 1)

            def fold_lo_part(e0, e1):
                for e in range(e0, e1):
                    dve.wait_ge(done["fold_hi"], e + 1)
                    o, hi = (t[:, e].rearrange("p k d -> p (k d)") for t in (fold_lo, fold_hi))
                    dve.tensor_tensor(o, bank[2 + e % 2][:, :], hi.bitcast(F32), ALU.subtract).then_inc(done["fold_lo"], 1)

            def split_lo(t_lo, t_hi, psum, s_hi, n, result):
                dve.wait_ge(s_hi, n)
                dve.tensor_tensor(t_lo, psum, t_hi.bitcast(F32), ALU.subtract).then_inc(result, 1)

            def patches_lo(n, tile):
                split_lo(flat(xT_lo[:, 3 * n:3 * n + 3, :]), flat(xT_hi[:, 3 * n:3 * n + 3, :]),
                         bank[n][:, 0:3 * TOK], done["xT_hi"], 2 * tile + n + 1, done["xT_lo"])

            def iteration(i, a, b, c):
                first = isinstance(i, int) and i == 0

                def experts(n):
                    dve.wait_ge(done["mm_f"], 4 * (i - 2) + n + 1)
                    for e in (2 * n, 2 * n + 1):
                        psum = bank[2 + n % 2][0:TOK, (e % 2) * DIM:(e % 2 + 1) * DIM]
                        which = 1 if e in (3, 5, 7) else 0
                        before = acc[:, which, :]
                        if e == 0:
                            before = h2[:]
                        elif e == 3:
                            dve.wait_ge(done["biases"], i - 1)
                            before = biases[:]
                        else:
                            dve.wait_ge(done["acc"], EXPERTS * (i - 2) + (e if e <= 2 else e - 1))
                        dve.scalar_tensor_tensor(acc[:, which, :], psum, hot[:, e:e + 1], before,
                                                 ALU.mult, ALU.add).then_inc(done["acc"], 1)

                def scores(n):
                    dve.wait_ge(done["mm_s"], 2 * (i - 1) + n + 1)
                    dve.wait_ge(done["sq"], 2 * (i - 1) + n + 1)
                    dve.tensor_tensor(flat(sc[:, n * HH:(n + 1) * HH, :]), bank[4 + n][0:TOK, 0:HALF],
                                      flat(sq[:, n * HH:(n + 1) * HH, :]), ALU.subtract).then_inc(done["sc"], 1)

                if first:
                    patches_lo(0, 0)
                    patches_lo(1, 0)
                    dve.wait_ge(done["bias1"], 1)
                    dve.wait_ge(done["extra"], 1)
                    dve.wait_ge(done["gamma2"], 1)
                if a:
                    dve.wait_ge(done["mm_y"], i + 1)
                    dve.tensor_tensor(y[:], bank[0][0:TOK, 0:DIM], bias1[:], ALU.add).then_inc(done["y"], 1)
                if c:
                    split_lo(flat(uT_lo[:]), flat(uT_hi[:]), bank[2][:, 0:KC * TOK], done["uT_hi"], i - 1,
                             done["uT_lo"])
                if a:
                    dve.wait_ge(done["y"], i + 1)
                    stats(y[:], st2[:], done["st2"], mv2, done["mv2"], ve2, done["ve2"], i + 1)
                    dve.scalar_tensor_tensor(yg[:], y[:], mv2[:, 0:1], gamma2[:],
                                             ALU.subtract, ALU.mult).then_inc(done["yg"], 1)
                    dve.wait_ge(done["rs2"], i + 1)
                    dve.wait_ge(done["yg"], i + 1)
                    free(dve, done["h_res"], i)
                    dve.scalar_tensor_tensor(h[:], yg[:], rs2[:], extra[:], ALU.mult, ALU.add).then_inc(done["h"], 1)
                    dve.wait_ge(done["h"], i + 1)
                    stats(h[:], st3[:], done["st3"], mv3, done["mv3"], ve3, done["ve3"], i + 1)
                if b:
                    scores(0)
                if a:
                    normalise(hn[:], h[:], mv3, rs3, done["rs3"], i + 1, done["hn"])
                if b:
                    scores(1)
                    dve.wait_ge(done["sc"], 2 * i)
                    dve.tensor_reduce(smax[:], sc[:], AX.X, ALU.max).then_inc(done["smax"], 1)
                if first:
                    rest_of_weights()
                if isinstance(i, int) and i < 2:
                    fold_lo_part(4 * i, 4 * i + 4)
                if c:
                    dve.wait_ge(done["mm_lg"], i - 1)
                    dve.tensor_tensor(logit[:], bank[3][0:TOK, 0:EXPERTS], row[:, R_GB:R_GB + EXPERTS], ALU.add)\
                        .then_inc(done["logit"], 1)
                    wait_apart(dve, done["logit"], i - 1, done["ve1"])
                    dve.max(top[:], logit[:]).then_inc(done["top"], 1)
                if a:
                    split_lo(flat(hT_lo[:]), flat(hT_hi[:]), bank[0][:, 0:KC * TOK], done["hT_hi"], i + 1,
                             done["hT_lo"])
                if c:
                    wait_apart(dve, done["top"], i - 1, done["ve1"])
                    dve.max_index(topi[:], top[:], logit[:]).then_inc(done["topi"], 1)
                    dve.wait_ge(done["topi"], i - 1)
                    dve.tensor_copy(topf[:], topi[:, 0:1]).then_inc(done["topf"], 1)
                    dve.wait_ge(done["topf"], i - 1)
                    dve.tensor_scalar(hot[:], iota8, topf[:], None, ALU.is_equal).then_inc(done["hot"], 1)
                    dve.wait_ge(done["hot"], i - 1)
                    free(dve, done["res"], i - 2)
                    experts(0)
                if b:
                    dve.wait_ge(done["ex"], i)
                    dve.tensor_reduce(ssum[:], ex[:], AX.X, ALU.add).then_inc(done["ssum"], 1)
                    dve.wait_ge(done["ssum"], i)
                    dve.reciprocal(rsum[:], ssum[:]).then_inc(done["rsum"], 1)
                if a:
                    dve.wait_ge(done["q"], i + 1)
                    dve.tensor_reduce(gsum[:], q[:].rearrange("p k (g t) -> p k g t", g=IMGS), AX.X, ALU.add)\
                        .then_inc(done["gsum"], 1)
                if c:
                    experts(1)
                if a:
                    dve.wait_ge(done["gsum"], i + 1)
                    dve.tensor_scalar(glo_hi[:], gsum[:], 1.0 / SEQ, None, ALU.mult).then_inc(done["glo_hi"], 1)
                    dve.wait_ge(done["glo_hi"], i + 1)
                    dve.scalar_tensor_tensor(glo_lo[:], gsum[:], 1.0 / SEQ, glo_hi[:].bitcast(F32),
                                             ALU.mult, ALU.subtract).then_inc(done["glo_lo"], 1)
                    dve.wait_ge(done["k_hi"], i + 1)
                    dve.tensor_tensor(k_s[:, 1], k[:], k_s[:, 0].bitcast(F32), ALU.subtract).then_inc(done["k_lo"], 1)
                    if has_next(i):
                        ln1(i + 2)
                        normalise(xn[:], xt[:], mv1, rs1, done["rs1"], i + 2, done["xn"])
                if b:
                    split_lo(flat(ctx_lo[:]), flat(ctx_hi[:]), bank[4][:, 0:KC * TOK], done["ctx_hi"], i,
                             done["ctx_lo"])
                if a and has_next(i):
                    patches_lo(0, i + 1)
                if c:
                    experts(2)
                if b:
                    dve.wait_ge(done["mm_o"], i)
                    dve.wait_ge(done["h_res"], i)
                    dve.tensor_tensor(h2[:], bank[5][0:TOK, 0:DIM], h_res[:], ALU.add).then_inc(done["h2"], 1)
                if a:
                    dve.wait_ge(done["epz"], i + 1)
                    dve.tensor_scalar(epz1[:], epz[:, HEADS:2 * HEADS], 1.0, None, ALU.add).then_inc(done["epz1"], 1)
                    dve.tensor_scalar(sp[:, 0:HEADS], epz[:, 0:HEADS], 1.0, ROOT2 / SEQ, ALU.add, ALU.mult)\
                        .then_inc(done["sps"], 1)
                if b:
                    dve.wait_ge(done["h2"], i)
                    stats(h2[:], st4[:], done["st4"], mv4, done["mv4"], ve4, done["ve4"], i)
                if a:
                    dve.wait_ge(done["epz1"], i + 1)
                    dve.reciprocal(rp[:], epz1[:]).then_inc(done["rp"], 1)
                    dve.wait_ge(done["sps"], i + 1)
                    dve.wait_ge(done["rp"], i + 1)
                    dve.scalar_tensor_tensor(sp[:, HEADS:2 * HEADS], sp[:, 0:HEADS], -float(SEQ), rp[:],
                                             ALU.mult, ALU.mult).then_inc(done["spn"], 1)
                if a and has_next(i):
                    patches_lo(1, i + 1)
                if a:
                    dve.wait_ge(done["spn"], i + 1)
                    dve.tensor_copy(sp4[:, 0:2 * HEADS], sp[:]).then_inc(done["sp_hi"], 1)
                    dve.wait_ge(done["sp_hi"], i + 1)
                    dve.tensor_tensor(sp4[:, 2 * HEADS:4 * HEADS], sp[:], sp4[:, 0:2 * HEADS].bitcast(F32), ALU.subtract)\
                        .then_inc(done["sp_lo"], 1)
                if b:
                    normalise(un[:], h2[:], mv4, rs4, done["rs4"], i, done["un"])
                if c:
                    experts(3)
                    dve.wait_ge(done["acc"], EXPERTS * (i - 1))
                    free(dve, done["stored"], 16 * (i - 2))
                    dve.tensor_tensor(res[:], acc[:, 0, :], acc[:, 1, :], ALU.add).then_inc(done["res"], 1)

            run(dve, iteration)


def _constants():
    c = np.zeros((128, C_END), np.float32)
    c[:, C_ID:C_ID + 128] = np.eye(128)
    omega = np.arange(DIM // 4, dtype=np.float32) / np.float32(DIM // 4 - 1)
    omega = (np.float32(1.0) / np.float32(10000.0) ** omega).astype(np.float32)
    yy, xx = np.meshgrid(np.arange(GRID), np.arange(GRID), indexing="ij")
    yo = yy.reshape(-1)[:, None].astype(np.float32) * omega[None]
    xo = xx.reshape(-1)[:, None].astype(np.float32) * omega[None]
    pe = np.concatenate((np.sin(xo), np.cos(xo), np.sin(yo), np.cos(yo)), axis=1)
    for g in range(IMGS):
        c[g * SEQ + 2:(g + 1) * SEQ, C_PE:C_PE + DIM] = pe
        c[g * SEQ + 2:(g + 1) * SEQ, C_MASK] = 1.0
        c[0, C_SEL + g * SEQ + 2:C_SEL + (g + 1) * SEQ] = 1.0
        c[1, C_SEL + g * SEQ] = 1.0
        c[2:4, C_SEL + g * SEQ + 1] = 1.0
    for hd in range(HEADS):
        at = slice(C_J + hd * SEQ, C_J + (hd + 1) * SEQ)
        for part in range(2):
            c[2 * HEADS * part + hd, at] = np.arange(SEQ)
            c[2 * HEADS * part + HEADS + hd, at] = 1.0
    c[:, C_IOTA:C_IOTA + EXPERTS] = np.arange(EXPERTS)
    return c


def kernel(**inputs):
    import concourse.bacc as bacc
    from concourse.bass_utils import run_bass_kernel_spmd

    t = {k: np.asarray(v) for k, v in inputs.items()}
    f = np.float32

    x = t["x"].reshape(BATCH, CH, GRID, PATCH, GRID, PATCH).transpose(0, 2, 4, 1, 3, 5).reshape(BATCH, GRID * GRID, PDIM)
    xr = np.zeros((TILES * IMGS, SEQ, PDIM), f)
    xr[:BATCH, 2:] = x

    def chunks(w):
        return w.reshape(-1, 128, *w.shape[1:]).swapaxes(0, 1)

    def patch_order(w):
        return w.reshape(PATCH * PATCH, CH, *w.shape[1:]).swapaxes(0, 1).reshape(PDIM, *w.shape[1:])

    cols = np.zeros((128, L_END), f)
    cols[:, L_G1:L_G1 + PC] = chunks(patch_order(t["L0_tok_ln1_g"]))
    cols[:, L_B1:L_B1 + PC] = chunks(patch_order(t["L0_tok_ln1_b"]))
    for at, name in ((L_BQ, "bq"), (L_BK, "bk"), (L_BFQ, "bfq"), (L_BFG, "bfg"), (L_BV, "bv")):
        cols[:, at:at + KC] = chunks(t["L0_attn_" + name])
    upz = np.zeros((DIM, 2 * HEADS), f)
    for hd in range(HEADS):
        upz[hd * HD:(hd + 1) * HD, hd] = t["L0_attn_uz"][hd, 0]
        upz[hd * HD:(hd + 1) * HD, HEADS + hd] = t["L0_attn_up"][hd, 0]
    cols[:, L_UPZ:L_UPZ + KC * 2 * HEADS] = chunks(upz).reshape(128, -1)
    cols[:, L_GATE:L_GATE + KC * EXPERTS] = chunks(t["L0_ffn_gate_w"]).reshape(128, -1)
    cols[:, L_EB:L_EB + HC * EXPERTS] = chunks(np.ascontiguousarray(t["L0_ffn_expert_b"].T)).reshape(128, -1)
    rows = np.concatenate([t["L0_tok_bias"], t["L0_tok_ln2_g"], t["L0_attn_bo"], t["L0_ffn_out_b"],
                           t["L0_ffn_gate_b"]])[None]
    heads4 = np.concatenate([t["L0_tok_ln2_b"][None], t["cls_tok"][0], t["L0_tok_cls_token"][0],
                             t["L0_tok_cls_pos_embedding"][0]])
    w_attn = np.stack([chunks(t["L0_attn_" + n]) for n in ("wq", "wk", "wv", "wfq", "wo", "wfg")], axis=1)
    w_exp = t["L0_ffn_expert_w"].transpose(2, 0, 1).reshape(HC, 128, EXPERTS, DIM).transpose(1, 0, 2, 3)

    arrays = {
        "x_in": xr.reshape(TILES * TOK, PDIM), "w_patch": chunks(patch_order(t["L0_tok_W"])), "w_attn": w_attn,
        "w_exp": w_exp, "w_out": chunks(t["L0_ffn_out_w"]), "consts": _constants(), "cols": cols, "rows": rows,
        "heads4": heads4,
    }
    nc = bacc.Bacc("TRN2", target_bir_lowering=False, num_devices=1)
    arrays = {k: np.ascontiguousarray(v) for k, v in arrays.items()}
    args = [nc.dram_tensor(k, v.shape, F32, kind="ExternalInput").ap() for k, v in arrays.items()]
    args.append(nc.dram_tensor("out", (TILES * TOK, DIM), F32, kind="ExternalOutput").ap())
    vit_tower(nc, *args)
    r = run_bass_kernel_spmd(nc, [arrays], core_ids=[0])
    return r.results[0]["out"][:BATCH * SEQ].reshape(BATCH, SEQ, DIM)
```

```python
import numpy as np
import concourse.bass as bass
from concourse import mybir
from concourse.alu_op_type import AluOpType as ALU
from contextlib import ExitStack

F32 = mybir.dt.float32
F32R = mybir.dt.float32r
U32 = mybir.dt.uint32
ACT = mybir.ActivationFunctionType
AX = mybir.AxisListType

BATCH, CH, IMG, PATCH = 32, 3, 96, 16
GRID = IMG // PATCH
DIM = 256
PDIM = CH * PATCH * PATCH
KC = DIM // 128
PC = PDIM // 128
SEQ = GRID * GRID + 2
HEADS, HD = 16, 16
HH = HEADS // 2
EXPERTS, HID = 8, 512
HC = HID // 128
IMGS = 3
TOK = IMGS * SEQ
TILES = -(-BATCH // IMGS)
EPS = 1e-5
PAIR = 2 * SEQ
HALF = HH * SEQ
ROOT2 = float(np.sqrt(2.0))

C_ID, C_PE, C_MASK, C_IOTA, C_SEL = 0, 128, 384, 385, 393
C_END = C_SEL + TOK
L_G1, L_B1, L_BQ, L_BK, L_BFQ, L_BFG, L_BV = 0, 6, 12, 14, 16, 18, 20
L_UPZ, L_GATE, L_EB = 22, 86, 102
L_END = L_EB + HC * EXPERTS
R_BIAS, R_G2, R_BO, R_OB, R_GB = 0, 256, 512, 768, 1024
R_END = 1032


def vit_tower(nc, x, w_patch, w_attn, w_exp, w_out, consts, j_values, cols, rows, heads4, out):
    es = ExitStack()
    with es:
        def sb(name, shape, dt=F32):
            return es.enter_context(nc.sbuf_tensor(name, shape, dt))

        def sem(name):
            return es.enter_context(nc.semaphore(name))

        cst = sb("cst", [128, C_END])
        col = sb("col", [128, L_END])
        row = sb("row", [TOK, R_END])
        head4 = sb("head4", [4, DIM])
        wp = sb("wp", [128, PC, DIM])
        wp_hi = sb("wp_hi", [128, PC, DIM], F32R)
        wp_lo = sb("wp_lo", [128, PC, DIM], F32R)
        wa = sb("wa", [128, 6, KC, DIM])
        wa_lo = sb("wa_lo", [128, 6, KC, DIM], F32R)
        wa_hi = sb("wa_hi", [128, 6, KC, DIM], F32R)
        WQ, WK, WV, WFQ, WO, WFG = range(6)
        gate_hi = sb("gate_hi", [128, KC, EXPERTS], F32R)
        gate_lo = sb("gate_lo", [128, KC, EXPERTS], F32R)
        wexp = sb("wexp", [128, 2, HC, DIM])
        wexp_hi = sb("wexp_hi", [128, 2, HC, DIM], F32R)
        wexp_lo = sb("wexp_lo", [128, 2, HC, DIM], F32R)
        wout = sb("wout", [128, HC, DIM])
        wout_hi = sb("wout_hi", [128, HC, DIM], F32R)
        wout_lo = sb("wout_lo", [128, HC, DIM], F32R)
        fold_hi = sb("fold_hi", [128, EXPERTS, KC, DIM], F32R)
        fold_lo = sb("fold_lo", [128, EXPERTS, KC, DIM], F32R)
        fbias_hi = sb("fbias_hi", [EXPERTS, DIM], F32R)
        fbias_lo = sb("fbias_lo", [EXPERTS, DIM], F32R)
        jmat = sb("jmat", [4 * HEADS, HEADS * SEQ], F32R)
        bias1 = sb("bias1", [TOK, DIM])
        extra = sb("extra", [TOK, DIM])
        bias_o = sb("bias_o", [TOK, DIM])
        nhalf = sb("nhalf", [TOK, 1])
        bk4 = sb("bk4", [128, KC])
        bf = sb("bf", [128, KC])
        xt = sb("xt", [TOK, PDIM])
        xn = sb("xn", [TOK, PDIM])
        st1 = sb("st1", [TOK, 2, 6])
        mv1 = sb("mv1", [TOK, 2])
        ve1 = sb("ve1", [TOK, 1])
        rs1 = sb("rs1", [TOK, 1])
        xT_hi = sb("xT_hi", [128, PC, TOK], F32R)
        xT_lo = sb("xT_lo", [128, PC, TOK], F32R)
        y = sb("y", [TOK, DIM])
        st2 = sb("st2", [TOK, 6])
        mv2 = sb("mv2", [TOK, 2])
        ve2 = sb("ve2", [TOK, 1])
        rs2 = sb("rs2", [TOK, 1])
        gamma2 = sb("gamma2", [TOK, DIM])
        yg = y
        h = sb("h", [TOK, DIM])
        h_res = sb("h_res", [TOK, DIM])
        st3 = sb("st3", [TOK, 6])
        mv3 = sb("mv3", [TOK, 2])
        ve3 = sb("ve3", [TOK, 1])
        rs3 = sb("rs3", [TOK, 1])
        hn = sb("hn", [TOK, DIM])
        hT_hi = sb("hT_hi", [128, KC, TOK], F32R)
        hT_lo = sb("hT_lo", [128, KC, TOK], F32R)
        qk = sb("qk", [TOK, 2, DIM])
        q = sb("q", [128, KC, TOK])
        q_hi = sb("q_hi", [128, KC, TOK], F32R)
        q_lo = sb("q_lo", [128, KC, TOK], F32R)
        q_bd = sb("q_bd", [128, 2 * KC, IMGS, TOK], F32R)
        k = sb("k", [128, KC, TOK])
        k_s = sb("k_s", [128, 2, KC, TOK], F32R)
        k_bd = sb("k_bd", [128, 2 * KC, HH, TOK], F32R)
        v_s = sb("v_s", [TOK, 2, HH, 2, HD])
        v_bd = sb("v_bd", [PAIR, IMGS, DIM])
        gsum = sb("gsum", [128, KC, IMGS])
        glo_hi = sb("glo_hi", [128, KC, IMGS, SEQ], F32R)
        glo_lo = sb("glo_lo", [128, KC, IMGS, SEQ], F32R)
        craw = sb("craw", [TOK, DIM])
        cth = sb("cth", [128, KC, TOK])
        epz = sb("epz", [TOK, 2 * HEADS])
        epz1 = sb("epz1", [TOK, HEADS])
        rp = sb("rp", [TOK, HEADS])
        sp = sb("sp", [TOK, 2 * HEADS])
        sp4 = sb("sp4", [TOK, 4 * HEADS], F32R)
        spT = sb("spT", [4 * HEADS, TOK], F32R)
        sq, sc = (wp[:].rearrange("p k d -> p (k d)")[0:TOK, n * HEADS * SEQ:(n + 1) * HEADS * SEQ]
                  .rearrange("p (h t) -> p h t", h=HEADS) for n in range(2))
        smax = sb("smax", [TOK, HEADS])
        sd = sb("sd", [TOK, HEADS, SEQ])
        ex = sd
        ssum = sb("ssum", [TOK, HEADS])
        rsum = sb("rsum", [TOK, HEADS])
        pr = sb("pr", [TOK, HEADS, SEQ])
        pT = wa[:].rearrange("p w k d -> p (w k d)")[0:PAIR, 2 * HC * DIM:2 * HC * DIM + HH * TOK]\
            .rearrange("p (j t) -> p j t", j=HH)
        ctx_hi = sb("ctx_hi", [128, KC, TOK], F32R)
        ctx_lo = sb("ctx_lo", [128, KC, TOK], F32R)
        h2 = sb("h2", [TOK, DIM])
        st4 = sb("st4", [TOK, 6])
        mv4 = sb("mv4", [TOK, 2])
        ve4 = sb("ve4", [TOK, 1])
        rs4 = sb("rs4", [TOK, 1])
        un = sb("un", [TOK, DIM])
        uT_hi = sb("uT_hi", [128, KC, TOK], F32R)
        uT_lo = sb("uT_lo", [128, KC, TOK], F32R)
        logit = sb("logit", [TOK, EXPERTS])
        top = sb("top", [TOK, 8])
        topi = sb("topi", [TOK, 8], U32)
        topf = sb("topf", [TOK, 1])
        hot = sb("hot", [TOK, EXPERTS])
        hotT = sb("hotT", [EXPERTS, TOK], F32R)
        acc = sb("acc", [TOK, 2, DIM])
        biases = wp[:].rearrange("p k d -> p (k d)")[0:TOK, 2 * HEADS * SEQ:2 * HEADS * SEQ + DIM]
        res = sb("res", [TOK, DIM])
        fold_bias = res[0:EXPERTS]

        bank = [es.enter_context(nc.psum_tensor(f"bank{i}", [128, 512], F32)) for i in range(8)]

        idtok = cst[0:TOK, C_ID:C_ID + TOK]
        pe_pos = cst[0:TOK, C_PE:C_PE + DIM]
        patch_mask = cst[0:TOK, C_MASK:C_MASK + 1]
        iota8 = cst[0:TOK, C_IOTA:C_IOTA + EXPERTS]
        sel4 = cst[0:4, C_SEL:C_SEL + TOK]
        upz = col[:, L_UPZ:L_UPZ + KC * 2 * HEADS].rearrange("p (k n) -> p k n", k=KC)
        gate = col[:, L_GATE:L_GATE + KC * EXPERTS].rearrange("p (k n) -> p k n", k=KC)
        ebT = col[:, L_EB:L_EB + HC * EXPERTS].rearrange("p (k n) -> p k n", k=HC)

        done = {name: sem("s_" + name) for name in """ld_cst ld_col ld_row ld_head4 ld_wp ld_wa ld_wout ld_j
            zeros nhalf bias_cols wp_hi wp_lo wa_hi wa_lo wb_lo gate_hi gate_lo jmat
            mm_bias1 mm_bias_o mm_extra mm_fb bias1 bias_o extra gamma2 fold_bias fbias_hi fbias_lo
            wexp_hi wexp_lo wout_hi wout_lo mm_fold fold_hi fold_lo table
            ld_x st1 mv1 ve1 rs1 xn mm_xT xT_hi xT_lo mm_y y st2 mv2 ve2 rs2 yg h h_res
            st3 mv3 ve3 rs3 hn mm_hT hT_hi hT_lo mm_qk qt kt q q_hi q_lo q_bd mm_k k k_hi k_lo k_bd
            mm_v v_s v_bd gsum glo_hi glo_lo mm_c craw mm_cT cth mm_pz epz epz1 rp sps spn sp_hi sp_lo mm_spT spT
            mm_g mm_s sq sc smax sd ex ssum rsum pr mm_pT pT mm_ctx ctx_hi ctx_lo mm_o h2
            st4 mv4 ve4 rs4 un mm_uT uT_hi uT_lo mm_lg logit top topi topf hot mm_f acc
            mm_hotT hotT mm_fbias biases res stored""".split()}

        ld_wexp = [sem(f"s_ld_wexp{n}") for n in range(EXPERTS // 2)]

        block = es.enter_context(nc.Block())

        def free(eng, semaphore, n):
            if not (isinstance(n, int) and n <= 0):
                eng.wait_ge(semaphore, n)

        def flat(t):
            return t.rearrange("p c t -> p (c t)")

        def diag(t, j):
            base = t[:, j, 0, 0:SEQ]
            return bass.AP(base.tensor, base.offset, [base.ap[0], [TOK + SEQ, IMGS], [1, SEQ]])

        def images(t, j):
            return t[:, j, :].rearrange("p (g t) -> p g t", g=IMGS)

        def means():
            return gsum[:].rearrange("p k g -> p (k g)").unsqueeze(2).to_broadcast([128, KC * IMGS, SEQ])

        def wait_apart(eng, semaphore, n, settled):
            if not isinstance(n, int):
                eng.wait_ge(settled, 1)
            eng.wait_ge(semaphore, n)

        def half(t, n):
            return t[:, n * HH:(n + 1) * HH]

        def to_keys(t, n):
            return half(t, n).unsqueeze(2).to_broadcast([TOK, HH, SEQ])

        def has_next(i):
            return not (isinstance(i, int) and i >= TILES - 1)

        def pair_weights(n):
            if n % 2 == 0:
                return wexp[:]
            return wa[:].rearrange("p w k d -> p (w k d)")[:, 0:2 * HC * DIM].rearrange("p (e j d) -> p e j d", e=2, j=HC)

        def fold_at(i, place):
            if not isinstance(i, int):
                return ()
            return {(0, "projected"): (0,), (0, "patches"): (1,), (0, "end"): (2,), (1, "patch product"): (3,),
                    (1, "tokens"): (4,), (1, "projected"): (5,), (1, "patches"): (6,), (1, "end"): (7,)}.get((i, place), ())

        def split_at(i, place):
            if not isinstance(i, int):
                return ()
            return {(0, "projected"): (2,), (0, "patches"): (3,), (0, "end"): (4,), (1, "patch product"): (5,),
                    (1, "tokens"): (6,), (1, "context"): (7,)}.get((i, place), ())

        def run(eng, iteration):
            iteration(0, True, False, False)
            iteration(1, True, True, False)
            iteration(2, True, True, True)
            with eng.Fori(3, TILES - 2) as i:
                iteration(i, True, True, True)
            iteration(TILES - 2, True, True, True)
            iteration(TILES - 1, True, True, True)
            iteration(TILES, False, True, True)
            iteration(TILES + 1, False, False, True)

        @block.sync
        def _(sync):
            sync.dma_start(xt[:], x[0:TOK, :]).then_inc(done["ld_x"], 16)
            sync.dma_start(wp[:], w_patch).then_inc(done["ld_wp"], 16)
            sync.wait_ge(done["xn"], 1)
            sync.dma_start(xt[:], x[TOK:2 * TOK, :]).then_inc(done["ld_x"], 16)
            sync.dma_start(wa[:], w_attn).then_inc(done["ld_wa"], 16)

            def load_experts(n):
                if n == 1:
                    sync.wait_ge(done["wa_lo"], 3)
                    sync.wait_ge(done["wb_lo"], 3)
                elif n > 1:
                    sync.wait_ge(done["wexp_lo"], 2 * n - 2)
                sync.dma_start(pair_weights(n), w_exp[:, 2 * n:2 * n + 2]).then_inc(ld_wexp[n], 16)

            for n in range(3):
                load_experts(n)

            def iteration(i, a, b, c):
                if a:
                    if isinstance(i, int) and i == 0:
                        sync.wait_ge(done["zeros"], 3)
                    sync.wait_ge(done["k_lo"], i + 1)
                    for hd in range(HH):
                        part = slice(hd * HD, (hd + 1) * HD)
                        sync.dma_start(
                            k_bd[part, :, hd, :].bitcast(F32),
                            k_s[part].rearrange("p a k t -> p (a k) t").bitcast(F32)).then_inc(done["k_bd"], 16)
                    if not (isinstance(i, int) and i >= TILES - 2):
                        patches = x[bass.ds((i + 2) * TOK, TOK), :]
                        sync.wait_ge(done["xn"], i + 2)
                        sync.dma_start(xt[:], patches).then_inc(done["ld_x"], 16)
                    free(sync, done["mm_ctx"], i)
                    sync.wait_ge(done["v_s"], i + 1)
                    for g in range(IMGS):
                        for par in range(2):
                            sync.dma_start(v_bd[par * SEQ:(par + 1) * SEQ, g, :],
                                           v_s[g * SEQ:(g + 1) * SEQ, par].rearrange("p a b d -> p (a b d)"))\
                                .then_inc(done["v_bd"], 16)
                if isinstance(i, int) and i == 0:
                    load_experts(3)
                if c:
                    sync.wait_ge(done["res"], i - 1)
                    sync.dma_start(out[bass.ds((i - 2) * TOK, TOK), :], res[:]).then_inc(done["stored"], 16)

            run(sync, iteration)
            sync.wait_ge(done["stored"], 16 * TILES)

        @block.gpsimd
        def _(pool):
            pool.dma_start(cst[:], consts).then_inc(done["ld_cst"], 16)
            pool.memset(nhalf[:], -0.5).then_inc(done["nhalf"], 1)
            pool.wait_ge(done["nhalf"], 1)

            def rstd(out_ap, in_ap, ready, result, n):
                pool.wait_ge(ready, n)
                pool.tensor_tensor(out_ap, in_ap, nhalf[:], ALU.pow).then_inc(result, 1)

            rstd(rs1[:], ve1[:], done["ve1"], done["rs1"], 1)
            pool.memset(q_bd[:].bitcast(F32), 0.0).then_inc(done["zeros"], 1)
            pool.memset(v_s[:], 0.0).then_inc(done["zeros"], 1)
            pool.memset(k_bd[:].bitcast(F32), 0.0).then_inc(done["zeros"], 1)

            def iteration(i, a, b, c):
                if a:
                    rstd(rs2[:], ve2[:], done["ve2"], done["rs2"], i + 1)
                    rstd(rs3[:], ve3[:], done["ve3"], done["rs3"], i + 1)
                if isinstance(i, int) and i == 0:
                    pool.wait_ge(done["mm_bias_o"], 1)
                    for j in (WFQ, WO, WFG):
                        pool.wait_ge(done["wa_hi"], j + 1)
                        pool.tensor_tensor(wa_lo[:, j], wa[:, j], wa_hi[:, j].bitcast(F32), ALU.subtract)\
                            .then_inc(done["wb_lo"], 1)
                if b:
                    for n in range(2):
                        pool.wait_ge(done["smax"], 2 * (i - 1) + n + 1)
                        pool.tensor_tensor(half(sd, n), half(sc, n), to_keys(smax, n), ALU.subtract)\
                            .then_inc(done["sd"], 1)
                    for n in range(2):
                        pool.wait_ge(done["rsum"], 2 * (i - 1) + n + 1)
                        if n == 0:
                            free(pool, done["mm_pT"], 2 * (i - 1))
                        pool.tensor_tensor(half(pr, n), half(ex, n), to_keys(rsum, n), ALU.mult)\
                            .then_inc(done["pr"], 1)
                if a:
                    pool.wait_ge(done["q_hi"], i + 1)
                    pool.tensor_tensor(q_lo[:], q[:], q_hi[:].bitcast(F32), ALU.subtract).then_inc(done["q_lo"], 1)
                    if has_next(i):
                        rstd(rs1[:], ve1[:], done["ve1"], done["rs1"], i + 2)
                if b:
                    rstd(rs4[:], ve4[:], done["ve4"], done["rs4"], i)
                if a:
                    if isinstance(i, int) and i == 0:
                        pool.wait_ge(done["bias_o"], 1)
                    pool.wait_ge(done["h"], i + 1)
                    free(pool, done["h2"], i)
                    pool.tensor_tensor(h_res[:], h[:], bias_o[:], ALU.add).then_inc(done["h_res"], 1)
                if c and not (isinstance(i, int) and i == TILES + 1):
                    pool.wait_ge(done["acc"], EXPERTS * (i - 1))
                    free(pool, done["stored"], 16 * (i - 2))
                    pool.tensor_tensor(res[:], acc[:, 0, :], acc[:, 1, :], ALU.add).then_inc(done["res"], 1)

            run(pool, iteration)

        @block.scalar
        def _(act):
            act.dma_start(col[:], cols).then_inc(done["ld_col"], 16)
            act.dma_start(row[:], rows.to_broadcast([TOK, R_END])).then_inc(done["ld_row"], 16)
            act.dma_start(head4[:], heads4).then_inc(done["ld_head4"], 16)
            act.dma_start(sd[0:4 * HEADS].rearrange("p h t -> p (h t)"), j_values).then_inc(done["ld_j"], 16)
            act.dma_start(wout[:], w_out).then_inc(done["ld_wout"], 16)

            act.wait_ge(done["nhalf"], 1)
            act.activation(epz[:, 0:1], nhalf[:], ACT.Exp).then_inc(done["table"], 1)

            act.wait_ge(done["ld_col"], 16)
            act.wait_ge(done["ld_wp"], 16)
            for j in range(PC):
                act.activation(wp_hi[:, j, :], wp[:, j, :], ACT.Copy,
                               scale=col[:, L_G1 + j:L_G1 + j + 1]).then_inc(done["wp_hi"], 1)

            def attention_weights():
                act.wait_ge(done["ld_wa"], 16)
                for j in range(6):
                    act.copy(wa_hi[:, j], wa[:, j]).then_inc(done["wa_hi"], 1)

            def rest_of_weights():
                act.copy(gate_hi[:], gate).then_inc(done["gate_hi"], 1)
                act.wait_ge(done["ld_j"], 16)
                act.copy(jmat[:], sd[0:4 * HEADS].rearrange("p h t -> p (h t)")).then_inc(done["jmat"], 1)
                act.wait_ge(done["ld_wout"], 16)
                act.copy(wout_hi[:], wout[:]).then_inc(done["wout_hi"], 1)
                expert_hi(0)
                expert_hi(1)

            def expert_hi(e):
                act.wait_ge(ld_wexp[e // 2], 16)
                if e >= 2:
                    act.wait_ge(done["mm_fold"], e - 1)
                    act.wait_ge(done["wexp_lo"], e - 1)
                act.copy(wexp_hi[:, e % 2], pair_weights(e // 2)[:, e % 2]).then_inc(done["wexp_hi"], 1)

            def fold(i, place):
                splits = list(split_at(i, place))
                for e in fold_at(i, place):
                    act.wait_ge(done["mm_fold"], e + 1)
                    act.copy(fold_hi[:, e].rearrange("p k d -> p (k d)"), bank[2 + e % 2][:, :]).then_inc(done["fold_hi"], 1)
                    if splits:
                        expert_hi(splits.pop(0))
                for e in splits:
                    expert_hi(e)

            def patches_hi(n, tile):
                act.wait_ge(done["mm_xT"], 2 * tile + n + 1)
                if n == 0:
                    free(act, done["mm_y"], tile)
                act.copy(flat(xT_hi[:, 3 * n:3 * n + 3, :]), bank[6 * n][:, 0:3 * TOK]).then_inc(done["xT_hi"], 1)

            def iteration(i, a, b, c):
                first = isinstance(i, int) and i == 0

                def exponentials():
                    for n in range(2):
                        act.wait_ge(done["sd"], 2 * (i - 1) + n + 1)
                        if n == 0:
                            free(act, done["pr"], 2 * (i - 1))
                        act.activation(half(ex, n), half(sd, n), ACT.Exp).then_inc(done["ex"], 1)

                def probabilities(n):
                    act.wait_ge(done["mm_pT"], 2 * (i - 1) + n + 1)
                    if n == 0:
                        free(act, done["mm_ctx"], i - 1)
                    act.copy(flat(pT[:, n * HH // 2:(n + 1) * HH // 2, :]), bank[6 + n][0:PAIR, 0:HH // 2 * TOK])\
                        .then_inc(done["pT"], 1)

                if first:
                    patches_hi(0, 0)
                    patches_hi(1, 0)
                    attention_weights()
                if b:
                    act.wait_ge(done["mm_spT"], i)
                    act.copy(spT[:], bank[7][0:4 * HEADS, 0:TOK]).then_inc(done["spT"], 1)
                if c:
                    act.wait_ge(done["mm_uT"], i - 1)
                    free(act, done["mm_f"], 4 * (i - 2))
                    act.copy(flat(uT_hi[:]), bank[2][:, 0:KC * TOK]).then_inc(done["uT_hi"], 1)
                if b:
                    for n in range(2):
                        act.wait_ge(done["mm_g"], 2 * (i - 1) + n + 1)
                        if n == 0:
                            free(act, done["sc"], 2 * (i - 1))
                        act.activation(flat(sq[:, n * HH:(n + 1) * HH, :]), bank[6 + n][0:TOK, 0:HALF], ACT.Square)\
                            .then_inc(done["sq"], 1)
                if isinstance(i, int) and i < 2:
                    fold(i, "patch product")
                if a:
                    act.wait_ge(done["mm_hT"], i + 1)
                    free(act, done["mm_v"], i)
                    act.copy(flat(hT_hi[:]), bank[0][:, 0:KC * TOK]).then_inc(done["hT_hi"], 1)
                if first:
                    rest_of_weights()
                if b:
                    exponentials()
                fold(i, "tokens")
                if a:
                    act.wait_ge(done["mm_qk"], i + 1)
                    for which, result in ((0, "qt"), (1, "kt")):
                        act.copy(qk[:, which], bank[1][0:TOK, which * DIM:(which + 1) * DIM]).then_inc(done[result], 1)
                    act.wait_ge(done["mm_v"], i + 1)
                    free(act, done["v_bd"], 6 * 16 * i)
                    pv = bank[0][0:TOK, 0:DIM].rearrange("p (a b d) -> p a b d", a=HH, b=2)
                    for par in range(2):
                        ins = act.copy(v_s[:, par, :, par, :], pv[:, :, par, :])
                    ins.then_inc(done["v_s"], 1)
                if c:
                    act.wait_ge(done["mm_hotT"], i - 1)
                    free(act, done["mm_fbias"], i - 2)
                    act.copy(hotT[:], bank[7][0:EXPERTS, 0:TOK]).then_inc(done["hotT"], 1)
                if a:
                    if first:
                        act.wait_ge(done["bias_cols"], 2)
                        act.wait_ge(done["zeros"], 3)
                    act.wait_ge(done["mm_k"], i + 1)
                    for m in range(KC):
                        ins = act.activation(q[:, m, :], bank[1][:, m * TOK:(m + 1) * TOK], ACT.Identity,
                                             bias=col[:, L_BQ + m:L_BQ + m + 1])
                    ins.then_inc(done["q"], 1)
                    act.wait_ge(done["q"], i + 1)
                    act.copy(q_hi[:], q[:]).then_inc(done["q_hi"], 1)
                    act.wait_ge(done["gsum"], i + 1)
                    act.activation(glo_hi[:].rearrange("p k g t -> p (k g) t"), means(), ACT.Copy, scale=1.0 / SEQ)\
                        .then_inc(done["glo_hi"], 1)
                    for m in range(KC):
                        ins = act.activation(k[:, m, :], bank[1][:, (KC + m) * TOK:(KC + m + 1) * TOK], ACT.Identity,
                                             bias=bk4[:, m:m + 1], scale=0.25)
                    ins.then_inc(done["k"], 1)
                    act.wait_ge(done["k"], i + 1)
                    free(act, done["k_bd"], 16 * HH * i)
                    act.copy(k_s[:, 0], k[:]).then_inc(done["k_hi"], 1)
                if b:
                    probabilities(0)
                    probabilities(1)
                if c:
                    act.wait_ge(done["mm_fbias"], i - 1)
                    free(act, done["res"], i - 2)
                    act.copy(biases, bank[5][0:TOK, 0:DIM]).then_inc(done["biases"], 1)
                fold(i, "projected")
                if a:
                    act.wait_ge(done["mm_c"], i + 1)
                    act.copy(craw[:], bank[0][0:TOK, 0:DIM]).then_inc(done["craw"], 1)
                if b:
                    act.wait_ge(done["mm_ctx"], i)
                    act.copy(flat(ctx_hi[:]), bank[4][:, 0:KC * TOK]).then_inc(done["ctx_hi"], 1)
                if a:
                    act.wait_ge(done["mm_cT"], i + 1)
                    for m in range(KC):
                        ins = act.activation(cth[:, m, :], bank[1][:, m * TOK:(m + 1) * TOK], ACT.Tanh, bias=bf[:, m:m + 1])
                    ins.then_inc(done["cth"], 1)
                    if has_next(i):
                        patches_hi(0, i + 1)
                        patches_hi(1, i + 1)
                    fold(i, "context")
                    fold(i, "patches")
                    act.wait_ge(done["mm_pz"], i + 1)
                    act.activation(epz[:], bank[4][0:TOK, DIM:DIM + 2 * HEADS], ACT.Exp, scale=-1.0).then_inc(done["epz"], 1)
                    if first:
                        act.wait_ge(done["zeros"], 3)
                    for part, t in enumerate((q_hi, q_lo)):
                        for j in range(KC):
                            ins = act.copy(diag(q_bd, KC * part + j), images(t.bitcast(F32), j))
                    ins.then_inc(done["q_bd"], 1)
                fold(i, "end")

            run(act, iteration)

        @block.tensor
        def _(pe):
            def mm3(o, left, right):
                last = len(left) - 1
                for n, ((lh, ll), (rh, rl)) in enumerate(zip(left, right)):
                    pe.matmul(o, lh, rh, start=(n == 0), stop=False)
                    pe.matmul(o, lh, rl, start=False, stop=False)
                    ins = pe.matmul(o, ll, rh, start=False, stop=(n == last))
                return ins

            def fixed_terms():
                pe.wait_ge(done["ld_col"], 16)
                pe.wait_ge(done["ld_wp"], 16)
                for j in range(PC):
                    ins = pe.matmul(bank[4][0:TOK, 0:DIM], col[:, L_B1 + j:L_B1 + j + 1].to_broadcast([128, TOK]),
                                    wp[:, j, :], start=(j == 0), stop=(j == PC - 1))
                ins.then_inc(done["mm_bias1"], 1)

            def biases_through():
                pe.wait_ge(done["ld_head4"], 16)
                pe.matmul(bank[3][0:TOK, 0:DIM], sel4, head4[:], start=True, stop=True).then_inc(done["mm_extra"], 1)
                pe.wait_ge(done["ld_wa"], 16)
                for j in range(KC):
                    ins = pe.matmul(bank[5][0:TOK, 0:DIM], col[:, L_BV + j:L_BV + j + 1].to_broadcast([128, TOK]),
                                    wa[:, WO, j, :], start=(j == 0), stop=(j == KC - 1))
                ins.then_inc(done["mm_bias_o"], 1)
                pe.wait_ge(done["ld_wout"], 16)
                for j in range(HC):
                    ins = pe.matmul(bank[7][0:EXPERTS, 0:DIM], ebT[:, j, :], wout[:, j, :],
                                    start=(j == 0), stop=(j == HC - 1))
                ins.then_inc(done["mm_fb"], 1)

            def fold(i, place):
                for e in fold_at(i, place):
                    if e == 0:
                        pe.wait_ge(done["wout_lo"], 1)
                    pe.wait_ge(done["wexp_lo"], e + 1)
                    if e >= 2:
                        pe.wait_ge(done["fold_lo"], e - 1)
                    for m in range(KC):
                        part = slice(m * 128, (m + 1) * 128)
                        ins = mm3(bank[2 + e % 2][:, m * DIM:(m + 1) * DIM],
                                  [(wexp_hi[:, e % 2, j, part], wexp_lo[:, e % 2, j, part]) for j in range(HC)],
                                  [(wout_hi[:, j, :], wout_lo[:, j, :]) for j in range(HC)])
                    ins.then_inc(done["mm_fold"], 1)

            def transpose_patches(n, tile):
                pe.wait_ge(done["xn"], tile + 1)
                for j in range(3):
                    ins = pe.transpose(bank[6 * n][:, j * TOK:(j + 1) * TOK],
                                       xn[:, (3 * n + j) * 128:(3 * n + j + 1) * 128], idtok)
                ins.then_inc(done["mm_xT"], 1)

            def iteration(i, a, b, c):
                first = isinstance(i, int) and i == 0
                hT = [(hT_hi[:, j, :], hT_lo[:, j, :]) for j in range(KC)]
                uT = [(uT_hi[:, j, :], uT_lo[:, j, :]) for j in range(KC)]

                def transpose(o, tokens, result):
                    for j in range(KC):
                        ins = pe.transpose(o[:, j * TOK:(j + 1) * TOK], tokens[:, j * 128:(j + 1) * 128], idtok)
                    if result:
                        ins.then_inc(result, 1)

                def experts(*which):
                    for e in which:
                        n = e // 2
                        ins = mm3(bank[2 + n % 2][0:TOK, (e % 2) * DIM:(e % 2 + 1) * DIM], uT,
                                  [(fold_hi[:, e, j, :], fold_lo[:, e, j, :]) for j in range(KC)])
                        if e % 2:
                            ins.then_inc(done["mm_f"], 1)

                if first:
                    pe.wait_ge(done["ld_cst"], 16)
                    transpose_patches(0, 0)
                    transpose_patches(1, 0)
                    fixed_terms()
                    pe.wait_ge(done["wp_lo"], PC)
                if a:
                    pe.wait_ge(done["xT_lo"], 2 * (i + 1))
                    mm3(bank[0][0:TOK, 0:DIM], [(xT_hi[:, j, :], xT_lo[:, j, :]) for j in range(PC)],
                        [(wp_hi[:, j, :], wp_lo[:, j, :]) for j in range(PC)]).then_inc(done["mm_y"], 1)
                if first:
                    biases_through()
                if b:
                    if isinstance(i, int) and i == 1:
                        pe.wait_ge(done["extra"], 1)
                        pe.wait_ge(done["fold_bias"], 1)
                        pe.wait_ge(done["jmat"], 1)
                    wait_apart(pe, done["sp_lo"], i, done["wout_lo"])
                    pe.transpose(bank[7][0:4 * HEADS, 0:TOK], sp4[:].bitcast(F32), idtok).then_inc(done["mm_spT"], 1)
                if c:
                    pe.wait_ge(done["un"], i - 1)
                    transpose(bank[2], un, done["mm_uT"])
                if b:
                    free(pe, done["h2"], i - 1)
                    pe.wait_ge(done["q_bd"], i)
                    pe.wait_ge(done["k_bd"], 16 * HH * i)
                    for n in range(2):
                        o = bank[4 + n][0:TOK, 0:HALF].rearrange("p (a b) -> p a b", a=HH)
                        keys = [tuple(k_bd[:, KC * w + n, :, g * SEQ:(g + 1) * SEQ] for w in range(2))
                                for g in range(IMGS)]
                        mm3(o, [(q_bd[:, n, g, :], q_bd[:, KC + n, g, :]) for g in range(IMGS)],
                            keys).then_inc(done["mm_s"], 1)
                        if n == 0:
                            pe.wait_ge(done["spT"], i)
                            for j in range(2):
                                pe.matmul(bank[6 + j][0:TOK, 0:HALF], spT[:], jmat[:, j * HALF:(j + 1) * HALF],
                                          start=True, stop=True).then_inc(done["mm_g"], 1)
                if c:
                    pe.wait_ge(done["uT_lo"], i - 1)
                    pe.wait_ge(done["sq"], 2 * i if b else 2 * TILES)
                    if isinstance(i, int) and i == 2:
                        pe.wait_ge(done["fold_lo"], EXPERTS)
                    mm3(bank[7][0:TOK, DIM:DIM + EXPERTS], uT,
                        [(gate_hi[:, j, :], gate_lo[:, j, :]) for j in range(KC)]).then_inc(done["mm_lg"], 1)
                    experts(0, 1)
                    free(pe, done["acc"], EXPERTS * (i - 2))
                    experts(2)
                fold(i, "patch product")
                if a:
                    pe.wait_ge(done["hn"], i + 1)
                    transpose(bank[0], hn, done["mm_hT"])
                fold(i, "tokens")
                if c:
                    experts(3)
                if a:
                    if first:
                        pe.wait_ge(done["wa_lo"], 2)
                    pe.wait_ge(done["hT_lo"], i + 1)
                    mm3(bank[1][0:TOK, 0:2 * DIM].rearrange("p (w d) -> p w d", w=2), hT,
                        [(wa_hi[:, WQ:WK + 1, j, :], wa_lo[:, WQ:WK + 1, j, :]) for j in range(KC)])\
                        .then_inc(done["mm_qk"], 1)
                    if first:
                        pe.wait_ge(done["wa_lo"], 3)
                    mm3(bank[0][0:TOK, 0:DIM], hT, [(wa_hi[:, WV, j, :], wa_lo[:, WV, j, :]) for j in range(KC)])\
                        .then_inc(done["mm_v"], 1)
                if c:
                    pe.wait_ge(done["hot"], i - 1)
                    pe.transpose(bank[7][0:EXPERTS, 0:TOK], hot[:], idtok).then_inc(done["mm_hotT"], 1)
                if a:
                    pe.wait_ge(done["kt"], i + 1)
                    transpose(bank[1], qk[:, 0], None)
                    transpose(bank[1][:, KC * TOK:], qk[:, 1], done["mm_k"])
                if c:
                    pe.wait_ge(done["acc"], EXPERTS * (i - 2) + 2)
                    experts(4)
                fold(i, "projected")
                if c:
                    pe.wait_ge(done["hotT"], i - 1)
                    pe.matmul(bank[5][0:TOK, 0:DIM], hotT[:], fbias_hi[:], start=True, stop=False)
                    pe.matmul(bank[5][0:TOK, 0:DIM], hotT[:], fbias_lo[:], start=False, stop=True)\
                        .then_inc(done["mm_fbias"], 1)
                if b:
                    for n in range(2):
                        pe.wait_ge(done["pr"], 2 * (i - 1) + n + 1)
                        for j in range(HH // 2):
                            pair = flat(pr[:, (n * HH + 2 * j):(n * HH + 2 * j + 2), :])
                            ins = pe.transpose(bank[6 + n][0:PAIR, j * TOK:(j + 1) * TOK], pair, idtok)
                        ins.then_inc(done["mm_pT"], 1)
                if c:
                    experts(5)
                if a:
                    pe.wait_ge(done["v_s"], i + 1)
                    pe.wait_ge(done["q_lo"], i + 1)
                    pe.wait_ge(done["glo_lo"], i + 1)
                    if first:
                        pe.wait_ge(done["wb_lo"], 3)
                    mm3(bank[0][0:TOK, 0:DIM], [(q_hi[:, j, :], q_lo[:, j, :]) for j in range(KC)] +
                        [tuple(t[:, j].rearrange("p g t -> p (g t)") for t in (glo_hi, glo_lo)) for j in range(KC)],
                        [(wa_hi[:, which, j, :], wa_lo[:, which, j, :]) for which in (WFQ, WFG) for j in range(KC)])\
                        .then_inc(done["mm_c"], 1)
                if b:
                    pe.wait_ge(done["v_bd"], 6 * 16 * i)
                    for j in range(HH):
                        if j % 4 == 0:
                            pe.wait_ge(done["pT"], 2 * (i - 1) + j // 4 + 1)
                        part = (j % 4) * 2 * HD
                        for g in range(IMGS):
                            at = (j // 4) * TOK + g * SEQ
                            ins = pe.matmul(bank[4][part:part + 2 * HD, at:at + SEQ],
                                            v_bd[:, g, j * 2 * HD:(j + 1) * 2 * HD],
                                            pT[:, j, g * SEQ:(g + 1) * SEQ], start=True, stop=True)
                    ins.then_inc(done["mm_ctx"], 1)
                if a:
                    pe.wait_ge(done["k"], i + 1)
                    pe.wait_ge(done["craw"], i + 1)
                    transpose(bank[1], craw, done["mm_cT"])
                    if has_next(i):
                        transpose_patches(0, i + 1)
                        transpose_patches(1, i + 1)
                    fold(i, "patches")
                if c:
                    pe.wait_ge(done["acc"], EXPERTS * (i - 2) + 4)
                    experts(6)
                if b:
                    if c:
                        pe.wait_ge(done["biases"], i - 1)
                    pe.wait_ge(done["ctx_lo"], i)
                    mm3(bank[5][0:TOK, 0:DIM], [(ctx_hi[:, j, :], ctx_lo[:, j, :]) for j in range(KC)],
                        [(wa_hi[:, WO, j, :], wa_lo[:, WO, j, :]) for j in range(KC)]).then_inc(done["mm_o"], 1)
                if a:
                    pe.wait_ge(done["cth"], i + 1)
                    for j in range(KC):
                        ins = pe.matmul(bank[4][0:TOK, DIM:DIM + 2 * HEADS], cth[:, j, :], upz[:, j, :],
                                        start=(j == 0), stop=(j == KC - 1))
                    ins.then_inc(done["mm_pz"], 1)
                if c:
                    experts(7)
                fold(i, "end")

            run(pe, iteration)

        @block.vector
        def _(dve):
            def stats(in_ap, st, s_st, mv, s_mv, ve, s_ve, n, between=None):
                dve.bn_stats(st, in_ap).then_inc(s_st, 1)
                if between:
                    between()
                wait_apart(dve, s_st, n, done["ve1"])
                dve.bn_aggr(mv[:], st).then_inc(s_mv, 1)
                dve.wait_ge(s_mv, n)
                dve.tensor_scalar(ve[:], mv[:, 1:2], EPS, None, ALU.add).then_inc(s_ve, 1)

            def normalise(o, in_ap, mv, rs, s_rs, n, result):
                dve.wait_ge(s_rs, n)
                dve.tensor_scalar(o, in_ap, mv[:, 0:1], rs[:], ALU.subtract, ALU.mult).then_inc(result, 1)

            def ln1(n, between=None):
                dve.wait_ge(done["ld_x"], 16 * n)
                for c in range(2):
                    ins = dve.bn_stats(st1[:, c, :], xt[:, c * 384:(c + 1) * 384])
                ins.then_inc(done["st1"], 1)
                if between:
                    between()
                wait_apart(dve, done["st1"], n, done["ve1"])
                dve.bn_aggr(mv1[:], st1[:].rearrange("p a b -> p (a b)")).then_inc(done["mv1"], 1)
                dve.wait_ge(done["mv1"], n)
                dve.tensor_scalar(ve1[:], mv1[:, 1:2], EPS, None, ALU.add).then_inc(done["ve1"], 1)

            ln1(1)
            dve.wait_ge(done["ld_col"], 16)
            dve.tensor_scalar(bk4[:], col[:, L_BK:L_BK + KC], 0.25, None, ALU.mult).then_inc(done["bias_cols"], 1)
            dve.tensor_tensor(bf[:], col[:, L_BFQ:L_BFQ + KC], col[:, L_BFG:L_BFG + KC], ALU.add)\
                .then_inc(done["bias_cols"], 1)
            normalise(xn[:], xt[:], mv1, rs1, done["rs1"], 1, done["xn"])
            dve.wait_ge(done["ld_wp"], 16)
            for j in range(PC):
                dve.wait_ge(done["wp_hi"], j + 1)
                dve.scalar_tensor_tensor(wp_lo[:, j, :], wp[:, j, :], col[:, L_G1 + j:L_G1 + j + 1],
                                         wp_hi[:, j, :].bitcast(F32), ALU.mult, ALU.subtract).then_inc(done["wp_lo"], 1)

            def fixed_terms():
                dve.wait_ge(done["ld_row"], 16)
                dve.wait_ge(done["ld_cst"], 16)
                dve.tensor_scalar(gamma2[:], row[:, R_G2:R_G2 + DIM], patch_mask, None, ALU.mult).then_inc(done["gamma2"], 1)
                dve.wait_ge(done["mm_bias1"], 1)
                dve.tensor_tensor(bias1[:], bank[4][0:TOK, 0:DIM], row[:, R_BIAS:R_BIAS + DIM], ALU.add)\
                    .then_inc(done["bias1"], 1)

            def attention_weights(*which):
                for j in which:
                    dve.wait_ge(done["wa_hi"], j + 1)
                    dve.tensor_tensor(wa_lo[:, j], wa[:, j], wa_hi[:, j].bitcast(F32), ALU.subtract)\
                        .then_inc(done["wa_lo"], 1)

            def weights_of_stage_c():
                dve.wait_ge(done["mm_bias_o"], 1)
                dve.tensor_tensor(bias_o[:], bank[5][0:TOK, 0:DIM], row[:, R_BO:R_BO + DIM], ALU.add)\
                    .then_inc(done["bias_o"], 1)
                dve.wait_ge(done["mm_fb"], 1)
                dve.tensor_tensor(fold_bias, bank[7][0:EXPERTS, 0:DIM], row[0:EXPERTS, R_OB:R_OB + DIM], ALU.add)\
                    .then_inc(done["fold_bias"], 1)
                dve.wait_ge(done["wout_hi"], 1)
                dve.tensor_tensor(wout_lo[:], wout[:], wout_hi[:].bitcast(F32), ALU.subtract).then_inc(done["wout_lo"], 1)
                expert_lo(0)

            def more_weights_of_stage_c():
                expert_lo(1)
                dve.wait_ge(done["fold_bias"], 1)
                dve.tensor_copy(fbias_hi[:], fold_bias).then_inc(done["fbias_hi"], 1)
                dve.wait_ge(done["fbias_hi"], 1)
                dve.tensor_tensor(fbias_lo[:], fold_bias, fbias_hi[:].bitcast(F32), ALU.subtract)\
                    .then_inc(done["fbias_lo"], 1)
                dve.tensor_tensor(gate_lo[:], gate, gate_hi[:].bitcast(F32), ALU.subtract).then_inc(done["gate_lo"], 1)

            def expert_lo(e):
                dve.wait_ge(done["wexp_hi"], e + 1)
                if e >= 2:
                    dve.wait_ge(done["mm_fold"], e - 1)
                dve.tensor_tensor(wexp_lo[:, e % 2], pair_weights(e // 2)[:, e % 2],
                                  wexp_hi[:, e % 2].bitcast(F32), ALU.subtract).then_inc(done["wexp_lo"], 1)

            def fold(i, place):
                for e in fold_at(i, place):
                    dve.wait_ge(done["fold_hi"], e + 1)
                    o, hi = (t[:, e].rearrange("p k d -> p (k d)") for t in (fold_lo, fold_hi))
                    dve.tensor_tensor(o, bank[2 + e % 2][:, :], hi.bitcast(F32), ALU.subtract).then_inc(done["fold_lo"], 1)
                for e in split_at(i, place):
                    expert_lo(e)

            def split_lo(t_lo, t_hi, psum, s_hi, n, result):
                dve.wait_ge(s_hi, n)
                dve.tensor_tensor(t_lo, psum, t_hi.bitcast(F32), ALU.subtract).then_inc(result, 1)

            def patches_lo(n, tile):
                split_lo(flat(xT_lo[:, 3 * n:3 * n + 3, :]), flat(xT_hi[:, 3 * n:3 * n + 3, :]),
                         bank[6 * n][:, 0:3 * TOK], done["xT_hi"], 2 * tile + n + 1, done["xT_lo"])

            def iteration(i, a, b, c):
                first = isinstance(i, int) and i == 0

                def experts(n, only=None):
                    if only is None or only == 2 * n:
                        dve.wait_ge(done["mm_f"], 4 * (i - 2) + n + 1)
                    for e in (2 * n, 2 * n + 1) if only is None else (only,):
                        psum = bank[2 + n % 2][0:TOK, (e % 2) * DIM:(e % 2 + 1) * DIM]
                        which = 1 if e in (3, 5, 7) else 0
                        before = acc[:, which, :]
                        if e == 0:
                            before = h2[:]
                        elif e == 3:
                            dve.wait_ge(done["biases"], i - 1)
                            before = biases
                        else:
                            dve.wait_ge(done["acc"], EXPERTS * (i - 2) + (e if e <= 2 else e - 1))
                        dve.scalar_tensor_tensor(acc[:, which, :], psum, hot[:, e:e + 1], before,
                                                 ALU.mult, ALU.add).then_inc(done["acc"], 1)

                def scores(n):
                    dve.wait_ge(done["mm_s"], 2 * (i - 1) + n + 1)
                    dve.wait_ge(done["sq"], 2 * (i - 1) + n + 1)
                    dve.tensor_tensor(flat(sc[:, n * HH:(n + 1) * HH, :]), bank[4 + n][0:TOK, 0:HALF],
                                      flat(sq[:, n * HH:(n + 1) * HH, :]), ALU.subtract).then_inc(done["sc"], 1)

                def means_of_q():
                    dve.wait_ge(done["q"], i + 1)
                    dve.tensor_reduce(gsum[:], q[:].rearrange("p k (g t) -> p k g t", g=IMGS), AX.X, ALU.add)\
                        .then_inc(done["gsum"], 1)

                def uT_lo_part():
                    if c:
                        split_lo(flat(uT_lo[:]), flat(uT_hi[:]), bank[2][:, 0:KC * TOK], done["uT_hi"], i - 1,
                                 done["uT_lo"])

                def maxima(n):
                    dve.wait_ge(done["sc"], 2 * (i - 1) + n + 1)
                    dve.tensor_reduce(half(smax, n), half(sc, n), AX.X, ALU.max).then_inc(done["smax"], 1)

                def maxima0():
                    if b:
                        maxima(0)
                    if first:
                        attention_weights(WQ)

                if first:
                    patches_lo(0, 0)
                    patches_lo(1, 0)
                    fixed_terms()
                    dve.wait_ge(done["bias1"], 1)
                    dve.wait_ge(done["gamma2"], 1)
                if a:
                    dve.wait_ge(done["mm_y"], i + 1)
                    dve.tensor_tensor(y[:], bank[0][0:TOK, 0:DIM], bias1[:], ALU.add).then_inc(done["y"], 1)
                    dve.wait_ge(done["y"], i + 1)
                    stats(y[:], st2[:], done["st2"], mv2, done["mv2"], ve2, done["ve2"], i + 1,
                          between=uT_lo_part)
                    dve.scalar_tensor_tensor(yg[:], y[:], mv2[:, 0:1], gamma2[:],
                                             ALU.subtract, ALU.mult).then_inc(done["yg"], 1)
                else:
                    uT_lo_part()
                if b:
                    scores(0)
                if a:
                    if first:
                        dve.wait_ge(done["mm_extra"], 1)
                        dve.tensor_tensor(extra[:], bank[3][0:TOK, 0:DIM], pe_pos, ALU.add).then_inc(done["extra"], 1)
                        dve.wait_ge(done["extra"], 1)
                    dve.wait_ge(done["rs2"], i + 1)
                    dve.wait_ge(done["yg"], i + 1)
                    free(dve, done["h_res"], i)
                    dve.scalar_tensor_tensor(h[:], yg[:], rs2[:], extra[:], ALU.mult, ALU.add).then_inc(done["h"], 1)
                    dve.wait_ge(done["h"], i + 1)
                    stats(h[:], st3[:], done["st3"], mv3, done["mv3"], ve3, done["ve3"], i + 1,
                          between=maxima0)
                    if first:
                        attention_weights(WK)
                else:
                    maxima0()
                if b:
                    scores(1)
                if c:
                    dve.wait_ge(done["mm_lg"], i - 1)
                    dve.tensor_tensor(logit[:], bank[7][0:TOK, DIM:DIM + EXPERTS], row[:, R_GB:R_GB + EXPERTS], ALU.add)\
                        .then_inc(done["logit"], 1)
                if a:
                    normalise(hn[:], h[:], mv3, rs3, done["rs3"], i + 1, done["hn"])
                if b:
                    maxima(1)
                if c:
                    wait_apart(dve, done["logit"], i - 1, done["ve1"])
                    dve.max(top[:], logit[:]).then_inc(done["top"], 1)
                if a:
                    split_lo(flat(hT_lo[:]), flat(hT_hi[:]), bank[0][:, 0:KC * TOK], done["hT_hi"], i + 1,
                             done["hT_lo"])
                if first:
                    attention_weights(WV)
                    weights_of_stage_c()
                fold(i, "patch product")
                fold(i, "tokens")
                if c:
                    wait_apart(dve, done["top"], i - 1, done["ve1"])
                    dve.max_index(topi[:], top[:], logit[:]).then_inc(done["topi"], 1)
                    dve.wait_ge(done["topi"], i - 1)
                    dve.tensor_copy(topf[:], topi[:, 0:1]).then_inc(done["topf"], 1)
                    dve.wait_ge(done["topf"], i - 1)
                    dve.tensor_scalar(hot[:], iota8, topf[:], None, ALU.is_equal).then_inc(done["hot"], 1)
                if b:
                    for n in range(2):
                        dve.wait_ge(done["ex"], 2 * (i - 1) + n + 1)
                        dve.tensor_reduce(half(ssum, n), half(ex, n), AX.X, ALU.add).then_inc(done["ssum"], 1)
                    for n in range(2):
                        dve.wait_ge(done["ssum"], 2 * (i - 1) + n + 1)
                        dve.reciprocal(half(rsum, n), half(ssum, n)).then_inc(done["rsum"], 1)
                if c:
                    dve.wait_ge(done["hot"], i - 1)
                    free(dve, done["res"], i - 2)
                    experts(0)
                if a and has_next(i):
                    ln1(i + 2, between=means_of_q)
                elif a:
                    means_of_q()
                if a:
                    dve.wait_ge(done["glo_hi"], i + 1)
                    dve.scalar_tensor_tensor(glo_lo[:].rearrange("p k g t -> p (k g) t"), means(), 1.0 / SEQ,
                                             glo_hi[:].rearrange("p k g t -> p (k g) t").bitcast(F32),
                                             ALU.mult, ALU.subtract).then_inc(done["glo_lo"], 1)
                if c:
                    experts(1, 2)
                if a:
                    dve.wait_ge(done["k_hi"], i + 1)
                    dve.tensor_tensor(k_s[:, 1], k[:], k_s[:, 0].bitcast(F32), ALU.subtract).then_inc(done["k_lo"], 1)
                    if has_next(i):
                        normalise(xn[:], xt[:], mv1, rs1, done["rs1"], i + 2, done["xn"])
                if c:
                    experts(1, 3)
                    experts(2)
                if first:
                    more_weights_of_stage_c()
                fold(i, "projected")
                if b:
                    split_lo(flat(ctx_lo[:]), flat(ctx_hi[:]), bank[4][:, 0:KC * TOK], done["ctx_hi"], i,
                             done["ctx_lo"])
                if a and has_next(i):
                    patches_lo(0, i + 1)
                    patches_lo(1, i + 1)
                fold(i, "context")
                fold(i, "patches")
                if b:
                    dve.wait_ge(done["mm_o"], i)
                    dve.wait_ge(done["h_res"], i)
                    dve.tensor_tensor(h2[:], bank[5][0:TOK, 0:DIM], h_res[:], ALU.add).then_inc(done["h2"], 1)
                if a:
                    dve.wait_ge(done["epz"], i + 1)
                    dve.tensor_scalar(epz1[:], epz[:, HEADS:2 * HEADS], 1.0, None, ALU.add).then_inc(done["epz1"], 1)
                    dve.tensor_scalar(sp[:, 0:HEADS], epz[:, 0:HEADS], 1.0, ROOT2 / SEQ, ALU.add, ALU.mult)\
                        .then_inc(done["sps"], 1)
                if b:
                    dve.wait_ge(done["h2"], i)
                    stats(h2[:], st4[:], done["st4"], mv4, done["mv4"], ve4, done["ve4"], i)
                if a:
                    dve.wait_ge(done["epz1"], i + 1)
                    dve.reciprocal(rp[:], epz1[:]).then_inc(done["rp"], 1)
                    dve.wait_ge(done["sps"], i + 1)
                    dve.wait_ge(done["rp"], i + 1)
                    dve.scalar_tensor_tensor(sp[:, HEADS:2 * HEADS], sp[:, 0:HEADS], -float(SEQ), rp[:],
                                             ALU.mult, ALU.mult).then_inc(done["spn"], 1)
                    dve.wait_ge(done["spn"], i + 1)
                    dve.tensor_copy(sp4[:, 0:2 * HEADS], sp[:]).then_inc(done["sp_hi"], 1)
                    dve.wait_ge(done["sp_hi"], i + 1)
                    dve.tensor_tensor(sp4[:, 2 * HEADS:4 * HEADS], sp[:], sp4[:, 0:2 * HEADS].bitcast(F32), ALU.subtract)\
                        .then_inc(done["sp_lo"], 1)
                if b:
                    normalise(un[:], h2[:], mv4, rs4, done["rs4"], i, done["un"])
                fold(i, "end")
                if c:
                    experts(3)
                if isinstance(i, int) and i == TILES + 1:
                    dve.wait_ge(done["acc"], EXPERTS * TILES)
                    dve.wait_ge(done["stored"], 16 * (i - 2))
                    dve.tensor_tensor(res[:], acc[:, 0, :], acc[:, 1, :], ALU.add).then_inc(done["res"], 1)

            run(dve, iteration)


def _constants():
    c = np.zeros((128, C_END), np.float32)
    jm = np.zeros((4 * HEADS, HEADS * SEQ), np.float32)
    c[:, C_ID:C_ID + 128] = np.eye(128)
    omega = np.arange(DIM // 4, dtype=np.float32) / np.float32(DIM // 4 - 1)
    omega = (np.float32(1.0) / np.float32(10000.0) ** omega).astype(np.float32)
    yy, xx = np.meshgrid(np.arange(GRID), np.arange(GRID), indexing="ij")
    yo = yy.reshape(-1)[:, None].astype(np.float32) * omega[None]
    xo = xx.reshape(-1)[:, None].astype(np.float32) * omega[None]
    pe = np.concatenate((np.sin(xo), np.cos(xo), np.sin(yo), np.cos(yo)), axis=1)
    for g in range(IMGS):
        c[g * SEQ + 2:(g + 1) * SEQ, C_PE:C_PE + DIM] = pe
        c[g * SEQ + 2:(g + 1) * SEQ, C_MASK] = 1.0
        c[0, C_SEL + g * SEQ + 2:C_SEL + (g + 1) * SEQ] = 1.0
        c[1, C_SEL + g * SEQ] = 1.0
        c[2:4, C_SEL + g * SEQ + 1] = 1.0
    for hd in range(HEADS):
        at = slice(hd * SEQ, (hd + 1) * SEQ)
        for part in range(2):
            jm[2 * HEADS * part + hd, at] = np.arange(SEQ)
            jm[2 * HEADS * part + HEADS + hd, at] = 1.0
    c[:, C_IOTA:C_IOTA + EXPERTS] = np.arange(EXPERTS)
    return c, jm


def kernel(**inputs):
    import concourse.bacc as bacc
    from concourse.bass_utils import run_bass_kernel_spmd

    t = {k: np.asarray(v) for k, v in inputs.items()}
    f = np.float32

    x = t["x"].reshape(BATCH, CH, GRID, PATCH, GRID, PATCH).transpose(0, 2, 4, 1, 3, 5).reshape(BATCH, GRID * GRID, PDIM)
    xr = np.zeros((TILES * IMGS, SEQ, PDIM), f)
    xr[:BATCH, 2:] = x

    def chunks(w):
        return w.reshape(-1, 128, *w.shape[1:]).swapaxes(0, 1)

    def patch_order(w):
        return w.reshape(PATCH * PATCH, CH, *w.shape[1:]).swapaxes(0, 1).reshape(PDIM, *w.shape[1:])

    cols = np.zeros((128, L_END), f)
    cols[:, L_G1:L_G1 + PC] = chunks(patch_order(t["L0_tok_ln1_g"]))
    cols[:, L_B1:L_B1 + PC] = chunks(patch_order(t["L0_tok_ln1_b"]))
    for at, name in ((L_BQ, "bq"), (L_BK, "bk"), (L_BFQ, "bfq"), (L_BFG, "bfg"), (L_BV, "bv")):
        cols[:, at:at + KC] = chunks(t["L0_attn_" + name])
    upz = np.zeros((DIM, 2 * HEADS), f)
    for hd in range(HEADS):
        upz[hd * HD:(hd + 1) * HD, hd] = t["L0_attn_uz"][hd, 0]
        upz[hd * HD:(hd + 1) * HD, HEADS + hd] = t["L0_attn_up"][hd, 0]
    cols[:, L_UPZ:L_UPZ + KC * 2 * HEADS] = chunks(upz).reshape(128, -1)
    cols[:, L_GATE:L_GATE + KC * EXPERTS] = chunks(t["L0_ffn_gate_w"]).reshape(128, -1)
    cols[:, L_EB:L_EB + HC * EXPERTS] = chunks(np.ascontiguousarray(t["L0_ffn_expert_b"].T)).reshape(128, -1)
    rows = np.concatenate([t["L0_tok_bias"], t["L0_tok_ln2_g"], t["L0_attn_bo"], t["L0_ffn_out_b"],
                           t["L0_ffn_gate_b"]])[None]
    heads4 = np.concatenate([t["L0_tok_ln2_b"][None], t["cls_tok"][0], t["L0_tok_cls_token"][0],
                             t["L0_tok_cls_pos_embedding"][0]])
    w_attn = np.stack([chunks(t["L0_attn_" + n]) for n in ("wq", "wk", "wv", "wfq", "wo", "wfg")], axis=1)
    w_exp = t["L0_ffn_expert_w"].transpose(2, 0, 1).reshape(HC, 128, EXPERTS, DIM).transpose(1, 2, 0, 3)

    consts, jm = _constants()
    arrays = {
        "x_in": xr.reshape(TILES * TOK, PDIM), "w_patch": chunks(patch_order(t["L0_tok_W"])), "w_attn": w_attn,
        "w_exp": w_exp, "w_out": chunks(t["L0_ffn_out_w"]), "consts": consts, "j_values": jm, "cols": cols, "rows": rows,
        "heads4": heads4,
    }
    nc = bacc.Bacc("TRN2", target_bir_lowering=False, num_devices=1)
    arrays = {k: np.ascontiguousarray(v) for k, v in arrays.items()}
    args = [nc.dram_tensor(k, v.shape, F32, kind="ExternalInput").ap() for k, v in arrays.items()]
    args.append(nc.dram_tensor("out", (TILES * TOK, DIM), F32, kind="ExternalOutput").ap())
    vit_tower(nc, *args)
    r = run_bass_kernel_spmd(nc, [arrays], core_ids=[0])
    return r.results[0]["out"][:BATCH * SEQ].reshape(BATCH, SEQ, DIM)
```
